# Optimizing a Trainium2 kernel written in Bass

```python
import numpy as np
import jax
import jax.numpy as jnp

def _softmax(x, axis=-1):
    return jax.nn.softmax(x, axis=axis)

def _gelu(x):
    return jax.nn.gelu(x, approximate=True)

def _silu(x):
    return jax.nn.silu(x)

def _sigmoid(x):
    return jax.nn.sigmoid(x)

def _layernorm(x, axis=-1, eps=1e-05):
    m = jnp.mean(x, axis=axis, keepdims=True)
    v = jnp.var(x, axis=axis, keepdims=True)
    return (x - m) / jnp.sqrt(v + eps)

def _scatter_add(tgt, idx, src, axis=0):
    return tgt.at[idx].add(src)

def _segment_sum(src, seg, n):
    return jax.ops.segment_sum(src, seg, n)
kernel_name = 'mk_flamingo_gated_d1_seqx_r8_bfdcf2'

def setup_inputs(seed: int=0):
    np.random.seed(seed)
    _w = jnp.asarray

    def _rec_inputs():
        import jax
        import jax.numpy as jnp
        _rk = jax.random.key(seed)
        x = 7.22e-05 + 1 * jax.random.normal(jax.random.fold_in(_rk, 1), (4, 256, 128), jnp.float32)
        _lenS = 256 - jax.random.randint(jax.random.fold_in(_rk, 7), (4,), 0, max(1, 256 // 4) + 1, jnp.int32)
        _lenS2 = 256 - jax.random.randint(jax.random.fold_in(_rk, 8), (4,), 0, max(1, 256 // 4) + 1, jnp.int32)
        _ctx_1024P = jax.random.normal(jax.random.fold_in(_rk, 11), (4, 16, 128), jnp.float32)
        _ctx_1024c = jax.random.dirichlet(jax.random.fold_in(_rk, 511), 0.3 * jnp.ones((16,), jnp.float32), (4, 256))
        _ctx_1024t = jnp.einsum('bsk,bkd->bsd', _ctx_1024c, _ctx_1024P)
        _ctx_1024t = _ctx_1024t * jax.lax.rsqrt(jnp.mean(jnp.square(_ctx_1024t)) + 1e-12) * 0.953939
        ctx_1024 = 4.13588e-05 + 0.999923 * (_ctx_1024t + 0.3 * jax.random.normal(jax.random.fold_in(_rk, 611), (4, 256, 128), jnp.float32))
        _g = jax.random.normal(jax.random.fold_in(_rk, 9001), (2, 1), jnp.float32)
        _g = jnp.sign(_g) * jnp.maximum(jnp.abs(_g), 1.0) + (_g == 0) * 1.0
        g_xattn = _g[0]
        g_ffn = _g[1]
        return (x, ctx_1024, g_xattn, g_ffn)
    x, ctx_1024, g_xattn, g_ffn = _rec_inputs()

    def _L0_xattn_setup():
        import jax, jax.numpy as jnp
        import numpy as np
        B, T, D, H = (4, 256, 128, 512)
        S = 32
        EPS = 1e-05

        def _layer_norm(x, gamma, beta):
            mu = jnp.mean(x, axis=-1, keepdims=True)
            var = jnp.mean(jnp.square(x - mu), axis=-1, keepdims=True)
            return (x - mu) * jax.lax.rsqrt(var + EPS) * gamma + beta

        def _aft_local(emb, wq, bq, wk, bk, wv, bv, wo, bo, pos_bias):
            q = emb @ wq + bq
            k = emb @ wk + bk
            v = emb @ wv + bv
            idx = jnp.arange(T)
            mask = (jnp.abs(idx[:, None] - idx[None, :]) < S).astype(pos_bias.dtype)
            w = pos_bias * mask
            max_k = jnp.max(k, axis=1, keepdims=True)
            max_w = jnp.max(w, axis=1, keepdims=True)
            ek = jnp.exp(k - max_k)
            ew = jnp.exp(w - max_w)
            num = jnp.einsum('tj,bjd->btd', ew, ek * v)
            den = jnp.einsum('tj,bjd->btd', ew, ek)
            y = jax.nn.sigmoid(q) * num / den
            return y @ wo + bo
        key = jax.random.key(seed)
        ks = jax.random.split(key, 16)
        sd = 0.02
        return {'x': jax.random.normal(ks[0], (B, T, D), jnp.float32), 'pos_encod': jax.random.normal(ks[1], (B, T, D), jnp.float32), 'wq': jax.random.normal(ks[2], (D, D), jnp.float32) * sd, 'bq': jnp.zeros((D,), jnp.float32), 'wk': jax.random.normal(ks[3], (D, D), jnp.float32) * sd, 'bk': jnp.zeros((D,), jnp.float32), 'wv': jax.random.normal(ks[4], (D, D), jnp.float32) * sd, 'bv': jnp.zeros((D,), jnp.float32), 'wo': jax.random.normal(ks[5], (D, D), jnp.float32) * sd, 'bo': jnp.zeros((D,), jnp.float32), 'pos_bias': jax.random.normal(ks[6], (T, T), jnp.float32) * sd, 'gamma': jnp.ones((D,), jnp.float32), 'beta': jnp.zeros((D,), jnp.float32), 'w1': jax.random.normal(ks[7], (D, H), jnp.float32) * sd, 'b1': jnp.zeros((H,), jnp.float32), 'w2': jax.random.normal(ks[8], (H, D), jnp.float32) * sd, 'b2': jnp.zeros((D,), jnp.float32)}
    _L0_xattn_all = _L0_xattn_setup()
    _L0_xattn_in = {k: v for k, v in _L0_xattn_all.items() if k in ('wq', 'bq', 'wk', 'bk', 'wv', 'bv', 'wo', 'bo', 'pos_bias', 'gamma', 'beta', 'w1', 'b1', 'w2', 'b2')}
    del _L0_xattn_all

    def _L0_ffn_setup():
        import jax, jax.numpy as jnp
        import numpy as np
        TOP_K = 2
        key = jax.random.key(seed)
        k1, k2, k3, k4 = jax.random.split(key, 4)
        B, T, D, H, E = (2, 256, 128, 256, 8)
        x = jax.random.normal(k1, (B, T, D), dtype=jnp.float32)
        w12 = jax.random.normal(k2, (E, 2 * H, D), dtype=jnp.float32) * D ** (-0.5)
        w3 = jax.random.normal(k3, (E, D, H), dtype=jnp.float32) * H ** (-0.5)
        gate_w = jax.random.normal(k4, (E, D), dtype=jnp.float32) * D ** (-0.5)
        return {'x': x, 'w12': w12, 'w3': w3, 'gate_w': gate_w}
    _L0_ffn_all = _L0_ffn_setup()
    _L0_ffn_in = {k: v for k, v in _L0_ffn_all.items() if k in ('w12', 'w3', 'gate_w')}
    del _L0_ffn_all
    return {'x': x, 'ctx_1024': ctx_1024, 'g_xattn': g_xattn, 'g_ffn': g_ffn, 'L0_xattn_wq': _L0_xattn_in['wq'], 'L0_xattn_bq': _L0_xattn_in['bq'], 'L0_xattn_wk': _L0_xattn_in['wk'], 'L0_xattn_bk': _L0_xattn_in['bk'], 'L0_xattn_wv': _L0_xattn_in['wv'], 'L0_xattn_bv': _L0_xattn_in['bv'], 'L0_xattn_wo': _L0_xattn_in['wo'], 'L0_xattn_bo': _L0_xattn_in['bo'], 'L0_xattn_pos_bias': _L0_xattn_in['pos_bias'], 'L0_xattn_gamma': _L0_xattn_in['gamma'], 'L0_xattn_beta': _L0_xattn_in['beta'], 'L0_xattn_w1': _L0_xattn_in['w1'], 'L0_xattn_b1': _L0_xattn_in['b1'], 'L0_xattn_w2': _L0_xattn_in['w2'], 'L0_xattn_b2': _L0_xattn_in['b2'], 'L0_ffn_w12': _L0_ffn_in['w12'], 'L0_ffn_w3': _L0_ffn_in['w3'], 'L0_ffn_gate_w': _L0_ffn_in['gate_w']}

def reference(x, ctx_1024, g_xattn, g_ffn, L0_xattn_wq, L0_xattn_bq, L0_xattn_wk, L0_xattn_bk, L0_xattn_wv, L0_xattn_bv, L0_xattn_wo, L0_xattn_bo, L0_xattn_pos_bias, L0_xattn_gamma, L0_xattn_beta, L0_xattn_w1, L0_xattn_b1, L0_xattn_w2, L0_xattn_b2, L0_ffn_w12, L0_ffn_w3, L0_ffn_gate_w):
    import jax
    import jax.numpy as jnp

    def _L0_xattn_ref(x, pos_encod, wq, bq, wk, bk, wv, bv, wo, bo, pos_bias, gamma, beta, w1, b1, w2, b2):
        import jax, jax.numpy as jnp
        import numpy as np
        B, T, D, H = (4, 256, 128, 512)
        S = 32
        EPS = 1e-05

        def _layer_norm(x, gamma, beta):
            mu = jnp.mean(x, axis=-1, keepdims=True)
            var = jnp.mean(jnp.square(x - mu), axis=-1, keepdims=True)
            return (x - mu) * jax.lax.rsqrt(var + EPS) * gamma + beta

        def _aft_local(emb, wq, bq, wk, bk, wv, bv, wo, bo, pos_bias):
            q = emb @ wq + bq
            k = emb @ wk + bk
            v = emb @ wv + bv
            idx = jnp.arange(T)
            mask = (jnp.abs(idx[:, None] - idx[None, :]) < S).astype(pos_bias.dtype)
            w = pos_bias * mask
            max_k = jnp.max(k, axis=1, keepdims=True)
            max_w = jnp.max(w, axis=1, keepdims=True)
            ek = jnp.exp(k - max_k)
            ew = jnp.exp(w - max_w)
            num = jnp.einsum('tj,bjd->btd', ew, ek * v)
            den = jnp.einsum('tj,bjd->btd', ew, ek)
            y = jax.nn.sigmoid(q) * num / den
            return y @ wo + bo
        emb = x + pos_encod
        attn = _aft_local(emb, wq, bq, wk, bk, wv, bv, wo, bo, pos_bias)
        a = _layer_norm(attn + emb, gamma, beta)
        ff = jax.nn.relu(a @ w1 + b1) @ w2 + b2
        return _layer_norm(ff + a, gamma, beta)

    def _L0_ffn_ref(x, w12, w3, gate_w):
        import jax, jax.numpy as jnp
        import numpy as np
        TOP_K = 2
        E = gate_w.shape[0]
        H = w3.shape[-1]
        scores = jnp.einsum('btd,ed->bte', x, gate_w)
        topk_scores, topk_idx = jax.lax.top_k(scores, TOP_K)
        topk_probs = jax.nn.softmax(topk_scores, axis=-1)
        total_probs = jnp.sum(jax.nn.one_hot(topk_idx, E, dtype=topk_probs.dtype) * topk_probs[..., None], axis=-2)
        h12 = jnp.einsum('btd,ehd->bteh', x, w12)
        h1, h2 = (h12[..., :H], h12[..., H:])
        hidden = jax.nn.silu(h1) * h2
        expert_out = jnp.einsum('bteh,edh->bted', hidden, w3)
        y = jnp.sum(total_probs[..., None] * expert_out, axis=-2)
        return y
    x = x + jnp.tanh(g_xattn[0]) * _L0_xattn_ref(_layernorm(x, axis=-1), ctx_1024, L0_xattn_wq, L0_xattn_bq, L0_xattn_wk, L0_xattn_bk, L0_xattn_wv, L0_xattn_bv, L0_xattn_wo, L0_xattn_bo, L0_xattn_pos_bias, L0_xattn_gamma, L0_xattn_beta, L0_xattn_w1, L0_xattn_b1, L0_xattn_w2, L0_xattn_b2)
    x = x + jnp.tanh(g_ffn[0]) * _L0_ffn_ref(_layernorm(x, axis=-1), L0_ffn_w12, L0_ffn_w3, L0_ffn_gate_w)
    return x

_drawn_inputs = setup_inputs


def setup_inputs(seed=0):
    import zlib

    import numpy as np

    out = dict(_drawn_inputs(seed))
    spreads = {'L0_xattn_bq': (0.0, 0.8),
     'L0_xattn_bk': (0.0, 2.0),
     'L0_xattn_bv': (0.0, 0.747),
     'L0_xattn_bo': (0.0, 0.1),
     'L0_xattn_gamma': (1.0, 0.2),
     'L0_xattn_beta': (0.0, 0.1),
     'L0_xattn_b1': (0.0, 0.351),
     'L0_xattn_b2': (0.0, 0.1)}
    factors = {'L0_xattn_wq': 8.0,
     'L0_xattn_wk': 8.0,
     'L0_xattn_wv': 4.927,
     'L0_xattn_wo': 4.251,
     'L0_xattn_pos_bias': 30.811}
    for name, (base, spread) in spreads.items():
        noise = np.random.default_rng([zlib.crc32(name.encode()), seed]).standard_normal(out[name].shape)
        drawn = base * np.exp(spread * noise) if base else spread * noise
        out[name] = jnp.asarray(drawn.astype(out[name].dtype))
    for name, factor in factors.items():
        out[name] = (out[name] * factor).astype(out[name].dtype)
    return out
```

```python
from contextlib import ExitStack

import concourse.bass as bass
from concourse import mybir
from concourse.alu_op_type import AluOpType as ALU

F32 = mybir.dt.float32
F32R = mybir.dt.float32r
U32 = mybir.dt.uint32
ACT = mybir.ActivationFunctionType
AX = mybir.AxisListType

P = 128
B, T, D = 4, 256, 128
N = B * T
TILES = N // P
TPB = T // P
HID = 512
HCH = HID // P
E = 8
EH = 256
ECH = EH // P
SPAN = 32
EPS = 1e-5
HALVES = 2
HALF = N // HALVES
HT = TILES // HALVES
UPH = E * ECH
UNITS = HALVES * UPH

LAG = 6
FIRST_UNIT = 13
LAST_STAGE = 15
POSITIONS = FIRST_UNIT + UNITS + 1

MAIN = [0, 2, 4, 5]
AUX = [1, 3, 4, 5]
H1_BANK, H2_BANK, Y_BANK = [0, 1], [2, 3], [6, 7]
EW_BANK = 7
SCORE_BANK, PT_BANK = [7, 4], [7, 5]

C_BQ, C_BK, C_BV, C_GAMMA, C_BETA, C_B1, C_GX, C_GF, C_IOTA = 0, 1, 2, 3, 4, 5, 9, 10, 11
N_COLS = C_IOTA + E
R_GAMMA, R_BETA, R_BO, R_B2, N_ROWS = 0, 1, 2, 3, 4
WQ, WK, WV, WO = 0, 1, 2, 3

WA_LOAD, W1_LOAD, W2_LOAD, EXPERT_LOAD = 0, 1, 2, 3
LOADS = EXPERT_LOAD + E
RAW_SLOTS = 4
EXPERT_COLS = 2 * EH + ECH * D


def build(nc, x_in, ctx_in, ident_in, cols_in, rows_in, pos_in, wa_in, w1_in, w2_in, gate_in, experts_in, out):
    with ExitStack() as stack:
        def sb(name, shape, dt=F32):
            return stack.enter_context(nc.sbuf_tensor(name, shape, dt))

        def sem(name):
            return stack.enter_context(nc.semaphore(name))

        x = sb("x", [P, TILES, D])
        cx = sb("cx", [P, TILES, D])
        ident = sb("ident", [P, P])
        cols = sb("cols", [P, N_COLS])
        rows = sb("rows", [P, N_ROWS, D])
        pos = sb("pos", [P, TPB, T])
        gate = sb("gate", [P, E])
        raw = sb("raw", [P, RAW_SLOTS, EXPERT_COLS])

        wa_hi, wa_lo = sb("wa_hi", [P, 4, D], F32R), sb("wa_lo", [P, 4, D], F32R)
        w1_hi, w1_lo = sb("w1_hi", [P, HID], F32R), sb("w1_lo", [P, HID], F32R)
        w2_hi, w2_lo = sb("w2_hi", [P, HCH, D], F32R), sb("w2_lo", [P, HCH, D], F32R)
        gate_hi, gate_lo = sb("gate_hi", [P, E], F32R), sb("gate_lo", [P, E], F32R)
        ex_hi, ex_lo = sb("ex_hi", [P, E, EXPERT_COLS], F32R), sb("ex_lo", [P, E, EXPERT_COLS], F32R)
        ewT_hi, ewT_lo = sb("ewT_hi", [P, TPB, T], F32R), sb("ewT_lo", [P, TPB, T], F32R)

        wmax, wneg = sb("wmax", [P, TPB]), sb("wneg", [P, TPB])
        st = sb("st", [P, 4, TILES, 6])
        mv = sb("mv", [P, 4, TILES, 2])
        ve = sb("ve", [P, 4, TILES])
        rstd = sb("rstd", [P, 4, TILES])
        mhalf = sb("mhalf", [P, TPB])
        kmax, kneg, kbias = sb("kmax", [P, B]), sb("kneg", [P, B]), sb("kbias", [P, B])
        negbq = sb("negbq", [P, 1])
        tx, tf = sb("tx", [P, 1]), sb("tf", [P, 1])
        halftf, neghalftf = sb("halftf", [P, 1]), sb("neghalftf", [P, 1])
        tgamma, tbeta, betab2 = sb("tgamma", [P, D]), sb("tbeta", [P, D]), sb("betab2", [P, D])

        emb = sb("emb", [P, TILES, D])
        embT_hi, embT_lo = sb("embT_hi", [P, 2, T], F32R), sb("embT_lo", [P, 2, T], F32R)
        ekT, ekvT, eq = sb("ekT", [P, 2, T]), sb("ekvT", [P, 2, T]), sb("eq", [P, 2, T])
        kv_hi, kv_lo = sb("kv_hi", [P, 2, TPB, 2, D], F32R), sb("kv_lo", [P, 2, TPB, 2, D], F32R)
        y = sb("y", [P, 2, T])
        y_hi, y_lo = sb("y_hi", [P, 2, T], F32R), sb("y_lo", [P, 2, T], F32R)
        z1 = sb("z1", [P, 2, TPB, D])
        res = sb("res", [P, 2, TPB, D])
        aT = sb("aT", [P, 2, T])
        aT_hi, aT_lo = sb("aT_hi", [P, 2, T], F32R), sb("aT_lo", [P, 2, T], F32R)
        hr = sb("hr", [P, 2, 2, T])
        hr_hi, hr_lo = sb("hr_hi", [P, 2, HCH, T], F32R), sb("hr_lo", [P, 2, HCH, T], F32R)
        xf = sb("xf", [P, 2, TPB, D])
        xfT_hi, xfT_lo = sb("xfT_hi", [P, N], F32R), sb("xfT_lo", [P, N], F32R)

        sc = sb("sc", [P, HT, E])
        top = sb("top", [P, HT, 8])
        topi = sb("topi", [P, HT, 8], U32)
        topf = sb("topf", [P, HT, 2])
        gap, tgap = sb("gap", [P, HT]), sb("tgap", [P, HT])
        pw = sb("pw", [P, 2, HT])
        chosen = sb("chosen", [P, 2, HT, E])
        probs = sb("probs", [P, HT, E])
        pT = sb("pT", [E, HALF])
        pall = sb("pall", [P, E, HALF])
        p_dram = nc.dram_tensor("p_dram", (HALVES, E, HALF), F32, kind="Internal").ap()

        hid = sb("hid", [P, 3, HALF])
        hid_hi, hid_lo = sb("hid_hi", [P, 3, HALF], F32R), sb("hid_lo", [P, 3, HALF], F32R)
        acc = sb("acc", [P, N])

        bank = [stack.enter_context(nc.psum_tensor(f"bank{i}", [P, 512], F32)) for i in range(8)]

        ld_x = [sem(f"ld_x{b}") for b in range(B)]
        ld_cx, ld_ident, ld_cols, ld_rows = sem("ld_cx"), sem("ld_ident"), sem("ld_cols"), sem("ld_rows")
        ld_pos, ld_gate = sem("ld_pos"), sem("ld_gate")
        ld_raw = [sem(f"ld_raw{s}") for s in range(RAW_SLOTS)]
        p_out, out_done = sem("p_out"), sem("out_done")
        p_back = [sem(f"p_back{e}") for e in range(E)]
        half_set, band_done, pre_done, wlo_done = sem("half_set"), sem("band_done"), sem("pre_done"), sem("wlo_done")
        rstd_done = [sem(f"rstd{k}_done") for k in range(4)]
        embbo_done, ylo_done, res_done = sem("embbo_done"), sem("ylo_done"), sem("res_done")
        hrlo_done, hidlo_done, xtb_done = sem("hrlo_done"), sem("hidlo_done"), sem("xtb_done")
        consts_done = sem("consts_done")
        wmax_done, wneg_done, ewlo_done = sem("wmax_done"), sem("wneg_done"), sem("ewlo_done")
        st_done = [sem(f"st{k}_done") for k in range(4)]
        mv_done = [sem(f"mv{k}_done") for k in range(4)]
        ve_done = [sem(f"ve{k}_done") for k in range(4)]
        xn_done, emb_done, embTlo_done = sem("xn_done"), sem("emb_done"), sem("embTlo_done")
        kmax_done, kneg_done, kbias_done, ekv_done = sem("kmax_done"), sem("kneg_done"), sem("kbias_done"), sem("ekv_done")
        kvlo_done, den_done, rden_done, y_done = sem("kvlo_done"), sem("den_done"), sem("rden_done"), sem("y_done")
        z1_done, n1_done, aTlo_done, hrhi_done = sem("z1_done"), sem("n1_done"), sem("aTlo_done"), sem("hrhi_done")
        z2_done, n2g_done, x1_done = sem("z2_done"), sem("n2g_done"), sem("x1_done")
        xf_done, xfTlo_done = sem("xf_done"), sem("xfTlo_done")
        sc_done, top_done, topi_done, topf_done = sem("sc_done"), sem("top_done"), sem("topi_done"), sem("topf_done")
        gap_done, pw_done, is_done, chosen_done = sem("gap_done"), sem("pw_done"), sem("is_done"), sem("chosen_done")
        probs_done, pT_done = sem("probs_done"), sem("pT_done")
        hid_done, yp_done, acc_done = sem("hid_done"), sem("yp_done"), sem("acc_done")
        gates_done, ew_done, ewhi_done, whi_done = sem("gates_done"), sem("ew_done"), sem("ewhi_done"), sem("whi_done")
        embThi_done, ek_done, eq_done, kvhi_done = sem("embThi_done"), sem("ek_done"), sem("eq_done"), sem("kvhi_done")
        yhi_done, aT_done, aThi_done, hr_done = sem("yhi_done"), sem("aT_done"), sem("aThi_done"), sem("hr_done")
        xfThi_done, x1T_done, tgap_done = sem("xfThi_done"), sem("x1T_done"), sem("tgap_done")
        silu_done, hidhi_done = sem("silu_done"), sem("hidhi_done")
        ewT_ready, embT_ready, kv_ready, q_ready = sem("ewT_ready"), sem("embT_ready"), sem("kv_ready"), sem("q_ready")
        kvT_ready, aft_ready, attn_ready, n1T_ready = sem("kvT_ready"), sem("aft_ready"), sem("attn_ready"), sem("n1T_ready")
        ff1_ready, ff2_ready, xfT_ready = sem("ff1_ready"), sem("ff2_ready"), sem("xfT_ready")
        sc_ready, pT_ready = sem("sc_ready"), sem("pT_ready")
        h1_ready, h2_ready, y_ready = sem("h1_ready"), sem("h2_ready"), sem("y_ready")

        def tok(b):
            return slice(TPB * b, TPB * b + TPB)

        def f32(ap):
            return ap.bitcast(F32)

        def ff_order(b, s):
            return 4 * (b // 2) + 2 * s + b % 2

        def raw_of(k):
            cols_of = EXPERT_COLS if k >= EXPERT_LOAD else 512
            return raw[:, k % RAW_SLOTS, 0:cols_of]

        def split_of(k):
            if k == WA_LOAD:
                return [t[:, :, :].rearrange("p a d -> p (a d)") for t in (wa_hi, wa_lo)]
            if k == W1_LOAD:
                return [t[:, :] for t in (w1_hi, w1_lo)]
            if k == W2_LOAD:
                return [t[:, :, :].rearrange("p a d -> p (a d)") for t in (w2_hi, w2_lo)]
            return [t[:, k - EXPERT_LOAD, :] for t in (ex_hi, ex_lo)]

        def raw_loaded(eng, k):
            eng.wait_ge(ld_raw[k % RAW_SLOTS], 16 * (k // RAW_SLOTS + 1))

        def stages_at(p):
            return ([(p, b) for b in (0, 1) if p <= LAST_STAGE]
                    + [(p - LAG, b) for b in (2, 3) if 0 <= p - LAG <= LAST_STAGE])

        block = stack.enter_context(nc.Block())

        @block.sync
        def _(sp):
            sp.dma_start(x[:, tok(0), :], x_in[:, tok(0), :]).then_inc(ld_x[0], 16)
            sp.dma_start(x[:, tok(1), :], x_in[:, tok(1), :]).then_inc(ld_x[1], 16)
            sp.dma_start(cx[:, :, :], ctx_in).then_inc(ld_cx, 16)
            weights = {WA_LOAD: wa_in, W1_LOAD: w1_in, W2_LOAD: w2_in}

            def load(k):
                if k >= RAW_SLOTS:
                    sp.wait_ge(wlo_done, k - RAW_SLOTS + 1)
                src = weights[k] if k in weights else experts_in[:, k - EXPERT_LOAD, :]
                sp.dma_start(raw_of(k), src).then_inc(ld_raw[k % RAW_SLOTS], 16)

            load(WA_LOAD)
            for b in (2, 3):
                sp.dma_start(x[:, tok(b), :], x_in[:, tok(b), :]).then_inc(ld_x[b], 16)
            for k in range(W1_LOAD, LOADS):
                load(k)
            for h in range(HALVES):
                sp.wait_ge(pT_done, h + 1)
                sp.dma_start(p_dram[h], pT[:, :]).then_inc(p_out, 16)
                sp.wait_ge(p_out, 16 * (h + 1))
                for e in range(E):
                    if h:
                        sp.wait_ge(acc_done, e + 1)
                    sp.dma_start(pall[:, e, :], p_dram[h, e, :].partition_broadcast(P)).then_inc(p_back[e], 16)
            sp.wait_ge(acc_done, E * HALVES)
            sp.dma_start(out[:, HALF:N], acc[:, HALF:N]).then_inc(out_done, 16)
            sp.wait_ge(out_done, 16 * HALVES)

        @block.gpsimd
        def _(pool):
            def inv_std(norm, b):
                pool.wait_ge(ve_done[norm], b + 1)
                pool.tensor_tensor(rstd[:, norm, tok(b)], ve[:, norm, tok(b)], mhalf[:, :],
                                   ALU.pow).then_inc(rstd_done[norm], 1)

            def split_low(k):
                hi, lo = split_of(k)
                pool.wait_ge(whi_done, k + 1)
                pool.tensor_tensor(lo, raw_of(k), f32(hi), ALU.subtract).then_inc(wlo_done, 1)

            def emb_with_bo(b):
                pool.wait_ge(emb_done, b + 1)
                pool.tensor_tensor(cx[:, tok(b), :], emb[:, tok(b), :],
                                   rows[:, R_BO:R_BO + 1, :].broadcast_to([P, TPB, D]),
                                   ALU.add).then_inc(embbo_done, 1)

            def x_with_beta(b):
                pool.wait_ge(xn_done, TPB * (b + 1))
                pool.tensor_tensor(x[:, tok(b), :], x[:, tok(b), :],
                                   tbeta[:, :].unsqueeze(1).broadcast_to([P, TPB, D]),
                                   ALU.add).then_inc(xtb_done, 1)

            def y_low(b):
                pool.wait_ge(yhi_done, b + 1)
                if b >= 2:
                    pool.wait_ge(attn_ready, b - 1)
                pool.tensor_tensor(y_lo[:, b % 2, :], y[:, b % 2, :], f32(y_hi[:, b % 2, :]),
                                   ALU.subtract).then_inc(ylo_done, 1)

            def residual(b):
                pool.wait_ge(n1_done, TPB * (b + 1))
                if b >= 2:
                    pool.wait_ge(x1_done, TPB * (b - 1))
                pool.tensor_tensor(res[:, b % 2, :, :], z1[:, b % 2, :, :],
                                   rows[:, R_GAMMA:R_GAMMA + 1, :].broadcast_to([P, TPB, D]),
                                   ALU.mult).then_inc(res_done, 1)
                pool.wait_ge(res_done, 2 * b + 1)
                pool.tensor_tensor(res[:, b % 2, :, :], res[:, b % 2, :, :],
                                   betab2[:, :].unsqueeze(1).broadcast_to([P, TPB, D]),
                                   ALU.add).then_inc(res_done, 1)

            def relu_low(b, s):
                pool.wait_ge(hrhi_done, ff_order(b, s) + 1)
                if b >= 2:
                    pool.wait_ge(ff2_ready, b - 1)
                pool.tensor_tensor(hr_lo[:, b % 2, 2 * s:2 * s + 2, :], hr[:, b % 2, :, :],
                                   f32(hr_hi[:, b % 2, 2 * s:2 * s + 2, :]), ALU.subtract).then_inc(hrlo_done, 1)

            def hidden_low(u):
                pool.wait_ge(hidhi_done, u + 1)
                if u >= 3:
                    pool.wait_ge(y_ready, u - 2)
                pool.tensor_tensor(hid_lo[:, u % 3, :], hid[:, u % 3, :], f32(hid_hi[:, u % 3, :]),
                                   ALU.subtract).then_inc(hidlo_done, 1)

            pool.memset(mhalf[:, :], -0.5).then_inc(half_set, 1)
            pool.wait_ge(half_set, 1)
            for p in range(POSITIONS):
                for stage, b in stages_at(p):
                    if stage == 0:
                        inv_std(0, b)
                    if stage == 1:
                        if b == 0:
                            pool.wait_ge(ld_rows, 16)
                        emb_with_bo(b)
                    if stage == 3:
                        x_with_beta(b)
                    if stage == 5:
                        y_low(b)
                    if stage == 6:
                        inv_std(1, b)
                    if stage == 7:
                        residual(b)
                    if stage in (8, 9):
                        relu_low(b, stage - 8)
                    if stage == 10:
                        inv_std(2, b)
                    if stage == 11:
                        inv_std(3, b)
                if p == 0:
                    pool.wait_ge(ld_pos, 16)
                    for r in range(TPB):
                        pool.affine_select(out=pos[:, r, :], in_=pos[:, r, :], compare_op=ALU.is_gt, fill=0.0,
                                           base=SPAN + P * r, pattern=[[-1, T]],
                                           channel_multiplier=1).then_inc(band_done, 1)
                    for r in range(TPB):
                        pool.wait_ge(band_done, r + 1)
                        pool.affine_select(out=pos[:, r, :], in_=pos[:, r, :], compare_op=ALU.is_gt, fill=0.0,
                                           base=SPAN - P * r, pattern=[[1, T]],
                                           channel_multiplier=-1).then_inc(band_done, 1)
                    split_low(WA_LOAD)
                if p == 1:
                    pool.wait_ge(gates_done, 2)
                    pool.tensor_scalar(tgamma[:, :], rows[:, R_GAMMA, :], tx[:, 0:1], None,
                                       ALU.mult).then_inc(pre_done, 1)
                    pool.tensor_scalar(tbeta[:, :], rows[:, R_BETA, :], tx[:, 0:1], None,
                                       ALU.mult).then_inc(pre_done, 1)
                    pool.tensor_tensor(betab2[:, :], rows[:, R_BETA, :], rows[:, R_B2, :],
                                       ALU.add).then_inc(pre_done, 1)
                    pool.wait_ge(pre_done, 3)
                if 1 <= p < LOADS:
                    split_low(p)
                if 0 <= p - FIRST_UNIT < UNITS:
                    hidden_low(p - FIRST_UNIT)

        @block.vector
        def _(dve):
            def stats(norm, b, src):
                for i in range(TPB):
                    t = TPB * b + i
                    dve.bn_stats(st[:, norm, t, :], src[:, i, :]).then_inc(st_done[norm], 1)
                for i in range(TPB):
                    t = TPB * b + i
                    dve.wait_ge(st_done[norm], t + 1)
                    dve.bn_aggr(mv[:, norm, t, :], st[:, norm, t, :]).then_inc(mv_done[norm], 1)
                dve.wait_ge(mv_done[norm], TPB * (b + 1))
                dve.tensor_scalar(ve[:, norm, tok(b)], mv[:, norm, tok(b), 1], EPS, None,
                                  ALU.add).then_inc(ve_done[norm], 1)

            def mean(norm, t):
                return mv[:, norm, t, 0:1]

            def inv(norm, t):
                return rstd[:, norm, t:t + 1]

            def ln_x_plus_ctx(b):
                dve.wait_ge(rstd_done[0], b + 1)
                for i in range(TPB):
                    t = TPB * b + i
                    dve.tensor_scalar(emb[:, t, :], x[:, t, :], mean(0, t), inv(0, t),
                                      ALU.subtract, ALU.mult).then_inc(xn_done, 1)
                if b == 0:
                    dve.wait_ge(ld_cx, 16)
                dve.wait_ge(xn_done, TPB * (b + 1))
                dve.tensor_tensor(emb[:, tok(b), :], emb[:, tok(b), :], cx[:, tok(b), :],
                                  ALU.add).then_inc(emb_done, 1)

            def embT_low(b):
                dve.wait_ge(embThi_done, b + 1)
                if b >= 2:
                    dve.wait_ge(q_ready, b - 1)
                dve.tensor_tensor(embT_lo[:, b % 2, :], bank[MAIN[b]][:, 0:T], f32(embT_hi[:, b % 2, :]),
                                  ALU.subtract).then_inc(embTlo_done, 1)

            def key_max(b):
                dve.wait_ge(kv_ready, b + 1)
                dve.tensor_reduce(kmax[:, b:b + 1], bank[AUX[b]][:, 0:T], AX.X, ALU.max).then_inc(kmax_done, 1)
                dve.wait_ge(kmax_done, b + 1)
                dve.tensor_scalar(kneg[:, b:b + 1], kmax[:, b:b + 1], cols[:, C_BK:C_BK + 1], -1.0,
                                  ALU.add, ALU.mult).then_inc(kneg_done, 1)
                dve.wait_ge(kneg_done, b + 1)
                dve.tensor_scalar(kbias[:, b:b + 1], kneg[:, b:b + 1], cols[:, C_BK:C_BK + 1], None,
                                  ALU.add).then_inc(kbias_done, 1)

            def key_times_value(b):
                dve.wait_ge(ek_done, b + 1)
                if b >= 2:
                    dve.wait_ge(kvT_ready, b - 1)
                dve.scalar_tensor_tensor(out=ekvT[:, b % 2, :], in0=bank[AUX[b]][:, T:2 * T],
                                         scalar=cols[:, C_BV:C_BV + 1], in1=ekT[:, b % 2, :],
                                         op0=ALU.add, op1=ALU.mult).then_inc(ekv_done, 1)

            def kv_low(b):
                dve.wait_ge(kvhi_done, b + 1)
                if b >= 2:
                    dve.wait_ge(aft_ready, b - 1)
                dve.tensor_tensor(kv_lo[:, b % 2, :, :, :].rearrange("p i k d -> p (i k d)"), bank[AUX[b]][:, :],
                                  f32(kv_hi[:, b % 2, :, :, :].rearrange("p i k d -> p (i k d)")),
                                  ALU.subtract).then_inc(kvlo_done, 1)

            def aft_out(b):
                s = b % 2
                dve.wait_ge(aft_ready, b + 1)
                if b >= 2:
                    dve.wait_ge(ylo_done, b - 1)
                dve.scalar_tensor_tensor(out=y[:, s, :], in0=eq[:, s, :], scalar=1.0, in1=bank[MAIN[b]][:, T:2 * T],
                                         op0=ALU.add, op1=ALU.mult).then_inc(den_done, 1)
                dve.wait_ge(den_done, b + 1)
                dve.reciprocal(y[:, s, :], y[:, s, :]).then_inc(rden_done, 1)
                dve.wait_ge(rden_done, b + 1)
                dve.tensor_tensor(y[:, s, :], y[:, s, :], bank[MAIN[b]][:, 0:T], ALU.mult).then_inc(y_done, 1)

            def attn_residual(b):
                dve.wait_ge(attn_ready, b + 1)
                dve.wait_ge(embbo_done, b + 1)
                if b >= 2:
                    dve.wait_ge(n1T_ready, b - 1)
                    dve.wait_ge(res_done, 2 * (b - 2) + 1)
                dve.tensor_tensor(z1[:, b % 2, :, :], bank[AUX[b]][:, 0:T].rearrange("p (i d) -> p i d", i=TPB),
                                  cx[:, tok(b), :], ALU.add).then_inc(z1_done, 1)
                dve.wait_ge(z1_done, b + 1)
                stats(1, b, z1[:, b % 2, :, :])

            def norm1(b):
                dve.wait_ge(rstd_done[1], b + 1)
                for i in range(TPB):
                    t = TPB * b + i
                    dve.tensor_scalar(z1[:, b % 2, i, :], z1[:, b % 2, i, :], mean(1, t), inv(1, t),
                                      ALU.subtract, ALU.mult).then_inc(n1_done, 1)

            def aT_low(b):
                dve.wait_ge(aThi_done, b + 1)
                if b >= 2:
                    dve.wait_ge(ff1_ready, ff_order(b - 2, 1) + 1)
                dve.tensor_tensor(aT_lo[:, b % 2, :], aT[:, b % 2, :], f32(aT_hi[:, b % 2, :]),
                                  ALU.subtract).then_inc(aTlo_done, 1)

            def relu_high(b, s):
                dve.wait_ge(hr_done, 2 * (ff_order(b, s) + 1))
                if b >= 2:
                    dve.wait_ge(ff2_ready, b - 1)
                dve.tensor_copy(hr_hi[:, b % 2, 2 * s:2 * s + 2, :], hr[:, b % 2, :, :]).then_inc(hrhi_done, 1)

            def ff_residual(b):
                dve.wait_ge(ff2_ready, b + 1)
                dve.wait_ge(res_done, 2 * (b + 1))
                dve.tensor_tensor(res[:, b % 2, :, :], bank[AUX[b]][:, 0:T].rearrange("p (i d) -> p i d", i=TPB),
                                  res[:, b % 2, :, :], ALU.add).then_inc(z2_done, 1)
                dve.wait_ge(z2_done, b + 1)
                stats(2, b, res[:, b % 2, :, :])

            def gated_x1(b):
                if b == 0:
                    dve.wait_ge(pre_done, 3)
                for i in range(TPB):
                    t = TPB * b + i
                    dve.scalar_tensor_tensor(out=res[:, b % 2, i, :], in0=res[:, b % 2, i, :], scalar=mean(2, t),
                                             in1=tgamma[:, :], op0=ALU.subtract, op1=ALU.mult).then_inc(n2g_done, 1)
                dve.wait_ge(rstd_done[2], b + 1)
                dve.wait_ge(xtb_done, b + 1)
                for i in range(TPB):
                    t = TPB * b + i
                    dve.wait_ge(n2g_done, t + 1)
                    dve.scalar_tensor_tensor(out=x[:, t, :], in0=res[:, b % 2, i, :], scalar=inv(2, t),
                                             in1=x[:, t, :], op0=ALU.mult, op1=ALU.add).then_inc(x1_done, 1)
                dve.wait_ge(x1_done, TPB * (b + 1))
                stats(3, b, x[:, tok(b), :])

            def norm3(b):
                dve.wait_ge(rstd_done[3], b + 1)
                if b >= 2:
                    dve.wait_ge(xfT_ready, b - 1)
                for i in range(TPB):
                    t = TPB * b + i
                    dve.tensor_scalar(xf[:, b % 2, i, :], x[:, t, :], mean(3, t), inv(3, t),
                                      ALU.subtract, ALU.mult).then_inc(xf_done, 1)

            def xfT_low(b):
                dve.wait_ge(xfThi_done, b + 1)
                if AUX[b] == MAIN[b]:
                    dve.wait_ge(x1T_done, b + 1)
                dve.tensor_tensor(xfT_lo[:, T * b:T * b + T], bank[MAIN[b]][:, 0:T],
                                  f32(xfT_hi[:, T * b:T * b + T]), ALU.subtract).then_inc(xfTlo_done, 1)

            def pick_top2(h):
                dve.wait_ge(sc_ready, h + 1)
                dve.tensor_copy(sc[:, :, :], bank[SCORE_BANK[h]][:, 0:HT * E].rearrange("p (t e) -> p t e", e=E)) \
                   .then_inc(sc_done, 1)
                dve.wait_ge(sc_done, h + 1)
                for t in range(HT):
                    dve.max(top[:, t, :], sc[:, t, :]).then_inc(top_done, 1)
                for t in range(HT):
                    dve.wait_ge(top_done, HT * h + t + 1)
                    dve.max_index(topi[:, t, :], top[:, t, :], sc[:, t, :]).then_inc(topi_done, 1)
                dve.tensor_tensor(gap[:, :], top[:, :, 0], top[:, :, 1], ALU.subtract).then_inc(gap_done, 1)
                dve.wait_ge(topi_done, HT * (h + 1))
                dve.tensor_copy(topf[:, :, :], topi[:, :, 0:2]).then_inc(topf_done, 1)
                dve.wait_ge(topf_done, h + 1)
                for k in range(2):
                    dve.tensor_tensor(chosen[:, k, :, :],
                                      cols[:, C_IOTA:C_IOTA + E].unsqueeze(1).broadcast_to([P, HT, E]),
                                      topf[:, :, k:k + 1].broadcast_to([P, HT, E]),
                                      ALU.is_equal).then_inc(is_done, 1)

            def route(h):
                dve.wait_ge(tgap_done, h + 1)
                for k, slope in ((0, halftf), (1, neghalftf)):
                    dve.tensor_scalar(pw[:, k, :], tgap[:, :], slope[:, 0:1], halftf[:, 0:1],
                                      ALU.mult, ALU.add).then_inc(pw_done, 1)
                for k in range(2):
                    dve.wait_ge(is_done, 2 * h + k + 1)
                    dve.wait_ge(pw_done, 2 * h + k + 1)
                    dve.tensor_tensor(chosen[:, k, :, :], chosen[:, k, :, :],
                                      pw[:, k, :].unsqueeze(2).broadcast_to([P, HT, E]),
                                      ALU.mult).then_inc(chosen_done, 1)
                dve.wait_ge(chosen_done, 2 * (h + 1))
                dve.tensor_tensor(probs[:, :, :], chosen[:, 0, :, :], chosen[:, 1, :, :],
                                  ALU.add).then_inc(probs_done, 1)

            def copy_pT(h):
                dve.wait_ge(pT_ready, h + 1)
                if h:
                    dve.wait_ge(p_out, 16 * h)
                dve.tensor_copy(pT[:, :], bank[PT_BANK[h]][0:E, :]).then_inc(pT_done, 1)

            def hidden(u):
                dve.wait_ge(silu_done, u + 1)
                dve.wait_ge(h2_ready, u + 1)
                dve.tensor_tensor(hid[:, u % 3, :], hid[:, u % 3, :], bank[H2_BANK[u % 2]][:, :],
                                  ALU.mult).then_inc(hid_done, 1)

            def add_expert(v):
                h, e = divmod(v, E)
                dve.wait_ge(y_ready, ECH * (v + 1))
                dve.wait_ge(p_back[e], 16 * (h + 1))
                dve.tensor_tensor(pall[:, e, :], pall[:, e, :], bank[Y_BANK[v % 2]][:, :],
                                  ALU.mult).then_inc(yp_done, 1)
                if e == 0:
                    dve.wait_ge(x1T_done, 2 * (h + 1))
                dve.wait_ge(yp_done, v + 1)
                if v:
                    dve.wait_ge(acc_done, v)
                dve.tensor_tensor(acc[:, HALF * h:HALF * h + HALF], acc[:, HALF * h:HALF * h + HALF],
                                  pall[:, e, :], ALU.add).then_inc(acc_done, 1)

            for p in range(POSITIONS):
                for stage, b in stages_at(p):
                    h = b // 2
                    if stage == 0:
                        dve.wait_ge(ld_x[b], 16)
                        stats(0, b, x[:, tok(b), :])
                    if stage == 1:
                        ln_x_plus_ctx(b)
                    if stage == 2:
                        embT_low(b)
                    if stage == 3:
                        if b == 0:
                            dve.wait_ge(ld_cols, 16)
                        key_max(b)
                    if stage == 4:
                        kv_low(b)
                    if stage == 5:
                        aft_out(b)
                    if stage == 6:
                        attn_residual(b)
                    if stage == 7:
                        norm1(b)
                        aT_low(b)
                    if stage in (8, 9):
                        relu_high(b, stage - 8)
                    if stage == 10:
                        ff_residual(b)
                    if stage == 11:
                        gated_x1(b)
                    if stage == 12:
                        norm3(b)
                        xfT_low(b)
                    if stage == 13 and b % 2:
                        pick_top2(h)
                    if stage == 14 and b % 2:
                        route(h)
                    if stage == 15 and b % 2:
                        copy_pT(h)
                for stage, b in stages_at(p):
                    if stage == 3:
                        key_times_value(b)
                if p == 1:
                    for r in range(TPB):
                        dve.wait_ge(band_done, TPB + r + 1)
                        dve.tensor_reduce(wmax[:, r:r + 1], pos[:, r, :], AX.X, ALU.max).then_inc(wmax_done, 1)
                    dve.wait_ge(wmax_done, TPB)
                    dve.tensor_scalar(wneg[:, :], wmax[:, :], -1.0, None, ALU.mult).then_inc(wneg_done, 1)
                    dve.wait_ge(ld_cols, 16)
                    dve.tensor_scalar(negbq[:, :], cols[:, C_BQ:C_BQ + 1], -1.0, None, ALU.mult).then_inc(consts_done, 1)
                    dve.wait_ge(gates_done, 2)
                    dve.tensor_scalar(halftf[:, :], tf[:, :], 0.5, None, ALU.mult).then_inc(consts_done, 1)
                    dve.tensor_scalar(neghalftf[:, :], tf[:, :], -0.5, None, ALU.mult).then_inc(consts_done, 1)
                if p == 3:
                    dve.wait_ge(ewhi_done, 1)
                    dve.tensor_tensor(ewT_lo[:, :, :].rearrange("p i t -> p (i t)"), bank[EW_BANK][:, :],
                                      f32(ewT_hi[:, :, :].rearrange("p i t -> p (i t)")),
                                      ALU.subtract).then_inc(ewlo_done, 1)
                    dve.wait_ge(ld_gate, 16)
                    dve.tensor_copy(gate_hi[:, :], gate[:, :]).then_inc(consts_done, 1)
                    dve.wait_ge(consts_done, 4)
                    dve.tensor_tensor(gate_lo[:, :], gate[:, :], f32(gate_hi[:, :]),
                                      ALU.subtract).then_inc(consts_done, 1)
                u = p - FIRST_UNIT
                if 0 <= u < UNITS:
                    hidden(u)
                if u >= 4 and u % 2 == 0:
                    add_expert((u - 4) // 2)
            for v in range((UNITS - 4) // 2 + 1, UNITS // 2):
                add_expert(v)

        @block.scalar
        def _(act):
            act.dma_start(ident[:, :], ident_in).then_inc(ld_ident, 16)
            act.dma_start(cols[:, :], cols_in).then_inc(ld_cols, 16)
            act.dma_start(pos[:, :, :], pos_in).then_inc(ld_pos, 16)
            act.dma_start(rows[:, :, :], rows_in).then_inc(ld_rows, 16)
            act.dma_start(gate[:, :], gate_in).then_inc(ld_gate, 16)

            def copy(dst, src):
                return act.activation(dst, src, ACT.Copy)

            def split_high(k):
                raw_loaded(act, k)
                copy(split_of(k)[0], raw_of(k)).then_inc(whi_done, 1)

            def embT_high(b):
                act.wait_ge(embT_ready, b + 1)
                if b >= 2:
                    act.wait_ge(q_ready, b - 1)
                copy(embT_hi[:, b % 2, :], bank[MAIN[b]][:, 0:T]).then_inc(embThi_done, 1)

            def exp_key(b):
                act.wait_ge(kbias_done, b + 1)
                if b >= 2:
                    act.wait_ge(kvT_ready, b - 1)
                act.activation(ekT[:, b % 2, :], bank[AUX[b]][:, 0:T], ACT.Exp,
                               bias=kbias[:, b:b + 1]).then_inc(ek_done, 1)

            def exp_query(b):
                act.wait_ge(q_ready, b + 1)
                if b >= 2:
                    act.wait_ge(den_done, b - 1)
                act.activation(eq[:, b % 2, :], bank[MAIN[b]][:, 0:T], ACT.Exp, bias=negbq[:, 0:1],
                               scale=-1.0).then_inc(eq_done, 1)

            def kv_high(b):
                act.wait_ge(kvT_ready, b + 1)
                if b >= 2:
                    act.wait_ge(aft_ready, b - 1)
                copy(kv_hi[:, b % 2, :, :, :].rearrange("p i k d -> p (i k d)"),
                     bank[AUX[b]][:, :]).then_inc(kvhi_done, 1)

            def y_high(b):
                act.wait_ge(y_done, b + 1)
                if b >= 2:
                    act.wait_ge(attn_ready, b - 1)
                copy(y_hi[:, b % 2, :], y[:, b % 2, :]).then_inc(yhi_done, 1)

            def a_transposed(b):
                act.wait_ge(n1T_ready, b + 1)
                if b >= 2:
                    act.wait_ge(aTlo_done, b - 1)
                act.activation(aT[:, b % 2, :], bank[MAIN[b]][:, 0:T], ACT.Identity,
                               bias=cols[:, C_BETA:C_BETA + 1], scale=cols[:, C_GAMMA:C_GAMMA + 1]) \
                   .then_inc(aT_done, 1)
                act.wait_ge(aT_done, b + 1)
                if b >= 2:
                    act.wait_ge(ff1_ready, ff_order(b - 2, 1) + 1)
                copy(aT_hi[:, b % 2, :], aT[:, b % 2, :]).then_inc(aThi_done, 1)

            def relu(b, s):
                n = ff_order(b, s)
                act.wait_ge(ff1_ready, n + 1)
                if n >= 2:
                    act.wait_ge(hrlo_done, n - 1)
                for c in range(2):
                    act.activation(hr[:, b % 2, c, :], bank[[AUX, MAIN][s][b]][:, T * c:T * c + T], ACT.Relu,
                                   bias=cols[:, C_B1 + 2 * s + c:C_B1 + 2 * s + c + 1]).then_inc(hr_done, 1)

            def xfT_high(b):
                act.wait_ge(xfT_ready, b + 1)
                copy(xfT_hi[:, T * b:T * b + T], bank[MAIN[b]][:, 0:T]).then_inc(xfThi_done, 1)
                copy(acc[:, T * b:T * b + T], bank[AUX[b]][:, T:2 * T]).then_inc(x1T_done, 1)

            for p in range(POSITIONS):
                for stage, b in stages_at(p):
                    if stage == 2:
                        embT_high(b)
                    if stage == 3:
                        exp_key(b)
                    if stage == 4:
                        exp_query(b)
                        kv_high(b)
                    if stage == 5:
                        y_high(b)
                    if stage == 7:
                        a_transposed(b)
                    if stage in (8, 9):
                        relu(b, stage - 8)
                    if stage == 12:
                        xfT_high(b)
                    if stage == 13 and b % 2:
                        act.wait_ge(gap_done, b // 2 + 1)
                        act.activation(tgap[:, :], gap[:, :], ACT.Tanh, scale=0.5).then_inc(tgap_done, 1)
                if p == 0:
                    act.wait_ge(ld_cols, 16)
                    act.activation(tx[:, :], cols[:, C_GX:C_GX + 1], ACT.Tanh).then_inc(gates_done, 1)
                    act.activation(tf[:, :], cols[:, C_GF:C_GF + 1], ACT.Tanh).then_inc(gates_done, 1)
                    split_high(WA_LOAD)
                if p == 1:
                    act.wait_ge(wneg_done, 1)
                    for r in range(TPB):
                        act.activation(pos[:, r, :], pos[:, r, :], ACT.Exp, bias=wneg[:, r:r + 1]).then_inc(ew_done, 1)
                if p == 2:
                    act.wait_ge(ewT_ready, 1)
                    copy(ewT_hi[:, :, :].rearrange("p i t -> p (i t)"), bank[EW_BANK][:, :]).then_inc(ewhi_done, 1)
                if 1 <= p < LOADS:
                    split_high(p)
                u = p - FIRST_UNIT
                if 0 <= u < UNITS:
                    act.wait_ge(h1_ready, u + 1)
                    if u >= 3:
                        act.wait_ge(hidlo_done, u - 2)
                    act.activation(hid[:, u % 3, :], bank[H1_BANK[u % 2]][:, :], ACT.Silu).then_inc(silu_done, 1)
                if 0 <= u - 1 < UNITS:
                    act.wait_ge(hid_done, u)
                    if u >= 4:
                        act.wait_ge(y_ready, u - 3)
                    copy(hid_hi[:, (u - 1) % 3, :], hid[:, (u - 1) % 3, :]).then_inc(hidhi_done, 1)
            act.wait_ge(acc_done, E)
            act.dma_start(out[:, 0:HALF], acc[:, 0:HALF]).then_inc(out_done, 16)

        @block.tensor
        def _(pe):
            def product(dst, w_hi, w_lo, m_hi, m_lo, first=True, last=True):
                pe.matmul(dst, w_hi, m_hi, start=first, stop=False)
                pe.matmul(dst, w_hi, m_lo, start=False, stop=False)
                return pe.matmul(dst, w_lo, m_hi, start=False, stop=last)

            def embT(b):
                pe.wait_ge(emb_done, b + 1)
                for i in range(TPB):
                    mm = pe.transpose(bank[MAIN[b]][:, P * i:P * i + P], emb[:, TPB * b + i, :], ident[:, :])
                mm.then_inc(embT_ready, 1)

            def project(dst, w, b):
                return product(dst, wa_hi[:, w, :], wa_lo[:, w, :], embT_hi[:, b % 2, :], embT_lo[:, b % 2, :])

            def keys_values(b):
                pe.wait_ge(wlo_done, WA_LOAD + 1)
                pe.wait_ge(embTlo_done, b + 1)
                project(bank[AUX[b]][:, 0:T], WK, b)
                project(bank[AUX[b]][:, T:2 * T], WV, b).then_inc(kv_ready, 1)

            def queries(b):
                if AUX[b] == MAIN[b]:
                    pe.wait_ge(ekv_done, b + 1)
                project(bank[MAIN[b]][:, 0:T], WQ, b).then_inc(q_ready, 1)

            def kvT(b):
                pe.wait_ge(ekv_done, b + 1)
                if AUX[b] == MAIN[b]:
                    pe.wait_ge(eq_done, b + 1)
                for i in range(TPB):
                    for k, src in enumerate((ekvT, ekT)):
                        mm = pe.transpose(bank[AUX[b]][:, P * (2 * i + k):P * (2 * i + k + 1)],
                                          src[:, b % 2, P * i:P * i + P], ident[:, :])
                mm.then_inc(kvT_ready, 1)

            def aft(b):
                if b == 0:
                    pe.wait_ge(ewlo_done, 1)
                pe.wait_ge(kvlo_done, b + 1)
                pe.wait_ge(eq_done, b + 1)
                for k in range(2):
                    for i in range(TPB):
                        mm = product(bank[MAIN[b]][:, T * k:T * k + T], kv_hi[:, b % 2, i, k, :],
                                     kv_lo[:, b % 2, i, k, :], ewT_hi[:, i, :], ewT_lo[:, i, :],
                                     first=(i == 0), last=(i == TPB - 1))
                mm.then_inc(aft_ready, 1)

            def attn(b):
                pe.wait_ge(ylo_done, b + 1)
                for i in range(TPB):
                    cut = slice(P * i, P * i + P)
                    mm = product(bank[AUX[b]][:, cut], y_hi[:, b % 2, cut], y_lo[:, b % 2, cut],
                                 wa_hi[:, WO, :], wa_lo[:, WO, :])
                mm.then_inc(attn_ready, 1)

            def n1T(b):
                pe.wait_ge(n1_done, TPB * (b + 1))
                for i in range(TPB):
                    mm = pe.transpose(bank[MAIN[b]][:, P * i:P * i + P], z1[:, b % 2, i, :], ident[:, :])
                mm.then_inc(n1T_ready, 1)

            def ff1(b, s):
                if s == 0:
                    pe.wait_ge(wlo_done, W1_LOAD + 1)
                    pe.wait_ge(aTlo_done, b + 1)
                elif AUX[b] == MAIN[b]:
                    pe.wait_ge(hr_done, 2 * (ff_order(b, 0) + 1))
                for c in range(2):
                    cut = slice(P * (2 * s + c), P * (2 * s + c) + P)
                    mm = product(bank[[AUX, MAIN][s][b]][:, T * c:T * c + T], w1_hi[:, cut], w1_lo[:, cut],
                                 aT_hi[:, b % 2, :], aT_lo[:, b % 2, :])
                mm.then_inc(ff1_ready, 1)

            def ff2(b):
                pe.wait_ge(wlo_done, W2_LOAD + 1)
                pe.wait_ge(hrlo_done, ff_order(b, 1) + 1)
                for i in range(TPB):
                    cut = slice(P * i, P * i + P)
                    for c in range(HCH):
                        mm = product(bank[AUX[b]][:, cut], hr_hi[:, b % 2, c, cut], hr_lo[:, b % 2, c, cut],
                                     w2_hi[:, c, :], w2_lo[:, c, :], first=(c == 0), last=(c == HCH - 1))
                mm.then_inc(ff2_ready, 1)

            def xfT(b):
                pe.wait_ge(xf_done, TPB * (b + 1))
                for i in range(TPB):
                    pe.transpose(bank[AUX[b]][:, T + P * i:T + P * i + P], x[:, TPB * b + i, :], ident[:, :])
                for i in range(TPB):
                    mm = pe.transpose(bank[MAIN[b]][:, P * i:P * i + P], xf[:, b % 2, i, :], ident[:, :])
                mm.then_inc(xfT_ready, 1)

            def scores(h):
                pe.wait_ge(consts_done, 5)
                pe.wait_ge(xfTlo_done, 2 * (h + 1))
                pe.wait_ge(x1T_done, 2 * (h + 1))
                for t in range(HT):
                    cut = slice(HALF * h + P * t, HALF * h + P * t + P)
                    mm = product(bank[SCORE_BANK[h]][:, E * t:E * t + E], xfT_hi[:, cut], xfT_lo[:, cut],
                                 gate_hi[:, :], gate_lo[:, :])
                mm.then_inc(sc_ready, 1)

            def probsT(h):
                pe.wait_ge(probs_done, h + 1)
                for t in range(HT):
                    mm = pe.transpose(bank[PT_BANK[h]][0:E, P * t:P * t + P], probs[:, t, :], ident[:, :])
                mm.then_inc(pT_ready, 1)

            def expert_in(u):
                h, e, c = u // UPH, u % UPH // ECH, u % ECH
                pe.wait_ge(wlo_done, EXPERT_LOAD + e + 1)
                pe.wait_ge(xfTlo_done, 2 * (h + 1))
                pe.wait_ge(x1T_done, 2 * (h + 1))
                tokens = slice(HALF * h, HALF * h + HALF)
                for part, (banks, freed, ready) in enumerate(((H1_BANK, silu_done, h1_ready),
                                                              (H2_BANK, hid_done, h2_ready))):
                    if u >= 2:
                        pe.wait_ge(freed, u - 1)
                    cut = slice(EH * part + P * c, EH * part + P * c + P)
                    product(bank[banks[u % 2]][:, :], ex_hi[:, e, cut], ex_lo[:, e, cut],
                            xfT_hi[:, tokens], xfT_lo[:, tokens]).then_inc(ready, 1)

            def expert_out(u):
                e, c, v = u % UPH // ECH, u % ECH, u // ECH
                pe.wait_ge(hidlo_done, u + 1)
                if v == 1:
                    pe.wait_ge(pT_done, 1)
                if v >= 2 and c == 0:
                    pe.wait_ge(yp_done, v - 1)
                cut = slice(2 * EH + D * c, 2 * EH + D * c + D)
                product(bank[Y_BANK[v % 2]][:, :], ex_hi[:, e, cut], ex_lo[:, e, cut],
                        hid_hi[:, u % 3, :], hid_lo[:, u % 3, :],
                        first=(c == 0), last=(c == ECH - 1)).then_inc(y_ready, 1)

            pe.wait_ge(ld_ident, 16)
            for p in range(POSITIONS):
                for stage, b in stages_at(p):
                    if stage == 1:
                        embT(b)
                    if stage == 2:
                        keys_values(b)
                    if stage == 3:
                        queries(b)
                    if stage == 4:
                        kvT(b)
                    if stage == 5:
                        aft(b)
                    if stage == 6:
                        attn(b)
                    if stage == 7:
                        n1T(b)
                    if stage in (8, 9):
                        ff1(b, stage - 8)
                    if stage == 10:
                        ff2(b)
                    if stage == 12:
                        xfT(b)
                    if stage == 13 and b % 2:
                        scores(b // 2)
                    if stage == 15 and b % 2:
                        probsT(b // 2)
                if p == 1:
                    pe.wait_ge(ew_done, TPB)
                    for i in range(TPB):
                        for r in range(TPB):
                            mm = pe.transpose(bank[EW_BANK][:, T * i + P * r:T * i + P * r + P],
                                              pos[:, r, P * i:P * i + P], ident[:, :])
                    mm.then_inc(ewT_ready, 1)
                u = p - FIRST_UNIT
                if 0 <= u < UNITS:
                    expert_in(u)
                if 0 <= u - 2 < UNITS:
                    expert_out(u - 2)
            expert_out(UNITS - 1)


def kernel(**inputs):
    import numpy as np
    import concourse.bacc as bacc
    from concourse import mybir as mb
    from concourse.bass_utils import run_bass_kernel_spmd

    g = {k: np.asarray(v) for k, v in inputs.items()}
    a = {k[len("L0_xattn_"):]: v for k, v in g.items() if k.startswith("L0_xattn_")}
    f = {k[len("L0_ffn_"):]: v for k, v in g.items() if k.startswith("L0_ffn_")}

    def token_rows(v):
        return v.reshape(TILES, P, D).transpose(1, 0, 2)

    def on_partitions(v):
        return v.reshape(-1, P).T

    iota = np.tile(np.arange(E, dtype=np.float32), (P, 1))
    cols = np.concatenate([on_partitions(a[n]) for n in ("bq", "bk", "bv", "gamma", "beta", "b1")]
                          + [np.tile(g[n].reshape(1, 1), (P, 1)) for n in ("g_xattn", "g_ffn")] + [iota], axis=1)
    rows = np.stack([np.tile(a[n], (P, 1)) for n in ("gamma", "beta", "bo", "b2")], axis=1)
    experts = np.concatenate([f["w12"].transpose(2, 0, 1),
                              f["w3"].reshape(E, D, ECH, P).transpose(3, 0, 2, 1).reshape(P, E, ECH * D)], axis=2)
    feeds = {
        "x_in": token_rows(g["x"]),
        "ctx_in": token_rows(g["ctx_1024"]),
        "ident_in": np.eye(P, dtype=np.float32),
        "cols_in": cols,
        "rows_in": rows,
        "pos_in": a["pos_bias"].reshape(TPB, P, T).transpose(1, 0, 2),
        "wa_in": np.concatenate([a[n] for n in ("wq", "wk", "wv", "wo")], axis=1),
        "w1_in": a["w1"],
        "w2_in": a["w2"].reshape(HCH, P, D).transpose(1, 0, 2).reshape(P, HCH * D),
        "gate_in": f["gate_w"].T,
        "experts_in": experts,
    }
    nc = bacc.Bacc("TRN2", target_bir_lowering=False, num_devices=1)
    feeds = {k: np.ascontiguousarray(v) for k, v in feeds.items()}
    aps = [nc.dram_tensor(k, v.shape, mb.dt.from_np(v.dtype), kind="ExternalInput").ap() for k, v in feeds.items()]
    out = nc.dram_tensor("out", (P, N), mb.dt.float32, kind="ExternalOutput").ap()
    build(nc, *aps, out)
    done = run_bass_kernel_spmd(nc, [feeds], core_ids=[0])
    return done.results[0]["out"].T.reshape(B, T, D)
```

```python
from contextlib import ExitStack

import concourse.bass as bass
from concourse import mybir
from concourse.alu_op_type import AluOpType as ALU

F32 = mybir.dt.float32
F32R = mybir.dt.float32r
U32 = mybir.dt.uint32
ACT = mybir.ActivationFunctionType
AX = mybir.AxisListType

P = 128
B, T, D = 4, 256, 128
N = B * T
TILES = N // P
TPB = T // P
HID = 512
HCH = HID // P
E = 8
EH = 256
ECH = EH // P
SPAN = 32
EPS = 1e-5
HALVES = 2
HALF = N // HALVES
HT = TILES // HALVES
UPH = E * ECH
UNITS = HALVES * UPH

STEP_AT = {
    "x stats": (0, 1, 9, 12),
    "emb": (2, 3, 20, 22),
    "keys and values": (4, 6, 27, 29),
    "key maximum": (10, 13, 30, 32),
    "query": (11, 14, 35, 36),
    "residual rows": (8, 16, 23, 26),
    "ek and ekv": (19, 21, 39, 40),
    "aft": (25, 28, 43, 46),
    "z1": (31, 33, 49, 51),
    "a": (41, 42, 56, 57),
    "feed forward 0": (44, 53, 62, 63),
    "feed forward 1": (48, 54, 66, 67),
    "z2": (50, 60, 73, 79),
    "z2 times gamma": (58, 65, 75, 82),
    "x1": (59, 68, 76, 89),
    "xf": (64, 69, 88, 94),
    "xf low": (71, 72, 91, 98),
    "scores": (74, 100),
    "route": (78, 101),
    "probs": (81, 104),
}
WEIGHTS_AT = {'band': 5, 'exp': 7, 'transposed': 17}
HI_AT = [18, 24, 37, 47, 52, 55, 83, 86]
LO_AT = [15, 34, 38, 45, 61, 70, 84, 90]
UNIT_AT = ([77, 80, 85, 87, 92, 93, 95, 96, 97, 99, 102, 103, 105, 106, 107, 108]
           + [109, 110, 111, 112, 113, 114, 115, 116, 117, 118, 119, 120, 121, 122, 123, 124])
OUT_LAG = 2
ADD_LAG = 4
HID_SLOTS = 4


def steps():
    timed = [(at, name, i) for name, ats in STEP_AT.items() for i, at in enumerate(ats)]
    timed += [(at, name, None) for name, at in WEIGHTS_AT.items()]
    timed += [(at, "split high", e) for e, at in enumerate(HI_AT)]
    timed += [(at, "split low", e) for e, at in enumerate(LO_AT)]
    timed += [(at, "unit", u) for u, at in enumerate(UNIT_AT)]
    timed += [(UNIT_AT[-1] + k, "unit", UNITS + k - 1) for k in range(1, ADD_LAG)]
    return [(name, i) for _, name, i in sorted(timed, key=lambda t: t[0])]


STEPS = steps()

MAIN = [0, 2, 4, 5]
AUX = [1, 3, 4, 5]
H1_BANK, H2_BANK, Y_BANK = [0, 1], [2, 3], [6, 7]
EW_BANK = 7
SCORE_BANK, PT_BANK = [7, 4], [7, 5]

C_BQ, C_BK, C_BV, C_BO, C_GAMMA, C_BETA, C_B2, C_B1, C_GX, C_GF, C_IOTA = 0, 1, 2, 3, 4, 5, 6, 7, 11, 12, 13
N_COLS = C_IOTA + E
R_GAMMA, R_BETA, R_BO, N_ROWS = 0, 1, 2, 3
WQ, WK, WV, WO = 0, 1, 2, 3

RAW_SLOTS = 3
EXPERT_COLS = 2 * EH + ECH * D


def build(nc, x_in, ctx_in, ident_in, cols_in, rows_in, pos_in, wa_in, w1_in, w2_in, gate_in, experts_in, out):
    with ExitStack() as stack:
        def sb(name, shape, dt=F32):
            return stack.enter_context(nc.sbuf_tensor(name, shape, dt))

        def sem(name):
            return stack.enter_context(nc.semaphore(name))

        x = sb("x", [P, TILES, D])
        cx = sb("cx", [P, TILES, D])
        ident = sb("ident", [P, P])
        cols = sb("cols", [P, N_COLS])
        rows = sb("rows", [P, N_ROWS, D])
        pos = sb("pos", [P, TPB, T])
        gate = sb("gate", [P, E])
        raw = sb("raw", [P, RAW_SLOTS, EXPERT_COLS])

        wa, w1, w2 = sb("wa", [P, 4, D]), sb("w1", [P, HID]), sb("w2", [P, HCH, D])
        ewT = sb("ewT", [P, TPB, T])
        ex_hi, ex_lo = sb("ex_hi", [P, E, EXPERT_COLS], F32R), sb("ex_lo", [P, E, EXPERT_COLS], F32R)

        wmax, wneg = sb("wmax", [P, TPB]), sb("wneg", [P, TPB])
        st = sb("st", [P, 4, TILES, 6])
        mv = sb("mv", [P, 4, TILES, 2])
        ve = sb("ve", [P, 4, TILES])
        rstd = sb("rstd", [P, 4, TILES])
        mhalf = sb("mhalf", [P, TPB])
        kmax, kneg, kbias = sb("kmax", [P, B]), sb("kneg", [P, B]), sb("kbias", [P, B])
        negbq, betab2 = sb("negbq", [P, 1]), sb("betab2", [P, 1])
        tx, tf = sb("tx", [P, 1]), sb("tf", [P, 1])
        halftf, neghalftf = sb("halftf", [P, 1]), sb("neghalftf", [P, 1])
        tgamma, tbeta = sb("tgamma", [P, D]), sb("tbeta", [P, D])

        emb = sb("emb", [P, TILES, D])
        embT = sb("embT", [P, B, T])
        ekT, ekvT, eq = sb("ekT", [P, B, T]), sb("ekvT", [P, B, T]), sb("eq", [P, B, T])
        kv = sb("kv", [P, B, TPB, 2, D])
        y = sb("y", [P, B, T])
        n1 = sb("n1", [P, B, TPB, D])
        aT, aTb = sb("aT", [P, B, T]), sb("aTb", [P, B, T])
        hr = sb("hr", [P, B, HCH, T])
        n2g = sb("n2g", [P, B, TPB, D])
        xf = sb("xf", [P, B, TPB, D])
        xfT = sb("xfT", [P, N])
        xfT_hi, xfT_lo = sb("xfT_hi", [P, N], F32R), sb("xfT_lo", [P, N], F32R)

        sc = sb("sc", [P, HT, E])
        top = sb("top", [P, HT, 8])
        topi = sb("topi", [P, HT, 8], U32)
        topf = sb("topf", [P, HT, 2])
        gap, tgap = sb("gap", [P, HT]), sb("tgap", [P, HT])
        pw = sb("pw", [P, 2, HT])
        chosen = sb("chosen", [P, 2, HT, E])
        probs = sb("probs", [P, HT, E])
        pT = sb("pT", [E, HALF])
        pall = sb("pall", [P, E, HALF])
        p_dram = nc.dram_tensor("p_dram", (HALVES, E, HALF), F32, kind="Internal").ap()

        hid = sb("hid", [P, HID_SLOTS, HALF])
        hid_hi, hid_lo = sb("hid_hi", [P, HID_SLOTS, HALF], F32R), sb("hid_lo", [P, HID_SLOTS, HALF], F32R)
        acc = sb("acc", [P, N])

        bank = [stack.enter_context(nc.psum_tensor(f"bank{i}", [P, 512], F32)) for i in range(8)]

        ld_x = [sem(f"ld_x{b}") for b in range(B)]
        ld_cx, ld_ident, ld_cols, ld_rows = sem("ld_cx"), sem("ld_ident"), sem("ld_cols"), sem("ld_rows")
        ld_pos, ld_gate, ld_wa, ld_w1, ld_w2 = sem("ld_pos"), sem("ld_gate"), sem("ld_wa"), sem("ld_w1"), sem("ld_w2")
        ld_raw = [sem(f"ld_raw{s}") for s in range(RAW_SLOTS)]
        p_out, out_done = sem("p_out"), sem("out_done")
        p_back = [sem(f"p_back{e}") for e in range(E)]
        half_set, band_done, pre_done, wlo_done = sem("half_set"), sem("band_done"), sem("pre_done"), sem("wlo_done")
        rstd_done = [sem(f"rstd{k}_done") for k in range(4)]
        hidlo_done, xtb_done, embb_done = sem("hidlo_done"), sem("xtb_done"), sem("embb_done")
        consts_done = sem("consts_done")
        wmax_done, wneg_done = sem("wmax_done"), sem("wneg_done")
        st_done = [sem(f"st{k}_done") for k in range(4)]
        mv_done = [sem(f"mv{k}_done") for k in range(4)]
        ve_done = [sem(f"ve{k}_done") for k in range(4)]
        xn_done, emb_done = sem("xn_done"), sem("emb_done")
        kmax_done, kneg_done, kbias_done, ekv_done = sem("kmax_done"), sem("kneg_done"), sem("kbias_done"), sem("ekv_done")
        den_done, rden_done, y_done = sem("den_done"), sem("rden_done"), sem("y_done")
        n1_done = sem("n1_done")
        n2g_done, x1_done = sem("n2g_done"), sem("x1_done")
        xf_done, xfTlo_done = sem("xf_done"), sem("xfTlo_done")
        sc_done, top_done, topi_done, topf_done = sem("sc_done"), sem("top_done"), sem("topi_done"), sem("topf_done")
        gap_done, pw_done, is_done, chosen_done = sem("gap_done"), sem("pw_done"), sem("is_done"), sem("chosen_done")
        probs_done, pT_done = sem("probs_done"), sem("pT_done")
        hid_done, yp_done, acc_done = sem("hid_done"), sem("yp_done"), sem("acc_done")
        gates_done, ew_done, ewT_done, whi_done = sem("gates_done"), sem("ew_done"), sem("ewT_done"), sem("whi_done")
        embT_done, ek_done, eq_done, kv_done = sem("embT_done"), sem("ek_done"), sem("eq_done"), sem("kv_done")
        aT_done = sem("aT_done")
        hr_done, ff1_ready = [sem(f"hr{b}_done") for b in range(B)], [sem(f"ff1_{b}_ready") for b in range(B)]
        aTb_done, b2_done = sem("aTb_done"), sem("b2_done")
        xfT_done, xfThi_done, x1T_done, tgap_done = sem("xfT_done"), sem("xfThi_done"), sem("x1T_done"), sem("tgap_done")
        silu_done, hidhi_done = sem("silu_done"), sem("hidhi_done")
        ewT_ready, embT_ready, kv_ready, q_ready = sem("ewT_ready"), sem("embT_ready"), sem("kv_ready"), sem("q_ready")
        kvT_ready, aft_ready, z1_ready = sem("kvT_ready"), sem("aft_ready"), sem("z1_ready")
        n1T_ready, z2_ready = sem("n1T_ready"), sem("z2_ready")
        xfT_ready = sem("xfT_ready")
        sc_ready, pT_ready = sem("sc_ready"), sem("pT_ready")
        h1_ready, h2_ready, y_ready = sem("h1_ready"), sem("h2_ready"), sem("y_ready")

        def tok(b):
            return slice(TPB * b, TPB * b + TPB)

        def f32(ap):
            return ap.bitcast(F32)

        block = stack.enter_context(nc.Block())

        @block.sync
        def _(sp):
            sp.dma_start(x[:, tok(0), :], x_in[:, tok(0), :]).then_inc(ld_x[0], 16)
            sp.dma_start(x[:, tok(1), :], x_in[:, tok(1), :]).then_inc(ld_x[1], 16)
            sp.dma_start(cx[:, :, :], ctx_in).then_inc(ld_cx, 16)
            sp.dma_start(wa[:, :, :], wa_in).then_inc(ld_wa, 16)
            for b in (2, 3):
                sp.dma_start(x[:, tok(b), :], x_in[:, tok(b), :]).then_inc(ld_x[b], 16)
            sp.dma_start(w1[:, :], w1_in).then_inc(ld_w1, 16)
            sp.dma_start(w2[:, :, :], w2_in).then_inc(ld_w2, 16)
            for e in range(E):
                if e >= RAW_SLOTS:
                    sp.wait_ge(wlo_done, e - RAW_SLOTS + 1)
                sp.dma_start(raw[:, e % RAW_SLOTS, :], experts_in[:, e, :]).then_inc(ld_raw[e % RAW_SLOTS], 16)
            for h in range(HALVES):
                sp.wait_ge(pT_done, h + 1)
                sp.dma_start(p_dram[h], pT[:, :]).then_inc(p_out, 16)
                sp.wait_ge(p_out, 16 * (h + 1))
                for e in range(E):
                    if h:
                        sp.wait_ge(acc_done, e + 1)
                    sp.dma_start(pall[:, e, :], p_dram[h, e, :].partition_broadcast(P)).then_inc(p_back[e], 16)
            sp.wait_ge(acc_done, E * HALVES)
            sp.dma_start(out[:, HALF:N], acc[:, HALF:N]).then_inc(out_done, 16)
            sp.wait_ge(out_done, 16 * HALVES)

        @block.gpsimd
        def _(pool):
            def inv_std(norm, b):
                pool.wait_ge(ve_done[norm], b + 1)
                pool.tensor_tensor(rstd[:, norm, tok(b)], ve[:, norm, tok(b)], mhalf[:, :],
                                   ALU.pow).then_inc(rstd_done[norm], 1)

            def split_low(e):
                pool.wait_ge(whi_done, e + 1)
                pool.tensor_tensor(ex_lo[:, e, :], raw[:, e % RAW_SLOTS, :], f32(ex_hi[:, e, :]),
                                   ALU.subtract).then_inc(wlo_done, 1)

            def x_with_beta(b):
                pool.wait_ge(pre_done, 2)
                pool.wait_ge(xn_done, TPB * (b + 1))
                pool.tensor_tensor(x[:, tok(b), :], x[:, tok(b), :],
                                   tbeta[:, :].unsqueeze(1).broadcast_to([P, TPB, D]),
                                   ALU.add).then_inc(xtb_done, 1)

            def emb_plus_bo(b):
                pool.wait_ge(embT_ready, b + 1)
                pool.tensor_tensor(emb[:, tok(b), :], emb[:, tok(b), :],
                                   rows[:, R_BO, :].unsqueeze(1).broadcast_to([P, TPB, D]),
                                   ALU.add).then_inc(embb_done, 1)

            def hidden_low(u):
                pool.wait_ge(hidhi_done, u + 1)
                s = u % HID_SLOTS
                if u >= HID_SLOTS:
                    pool.wait_ge(y_ready, u - HID_SLOTS + 1)
                pool.tensor_tensor(hid_lo[:, s, :], hid[:, s, :], f32(hid_hi[:, s, :]),
                                   ALU.subtract).then_inc(hidlo_done, 1)

            pool.memset(mhalf[:, :], -0.5).then_inc(half_set, 1)
            pool.wait_ge(half_set, 1)
            for step, i in STEPS:
                if step == "x stats":
                    inv_std(0, i)
                if step == "residual rows":
                    emb_plus_bo(i)
                    x_with_beta(i)
                if step == "z1":
                    inv_std(1, i)
                if step == "z2":
                    inv_std(2, i)
                if step == "x1":
                    inv_std(3, i)
                if step == "split low":
                    split_low(i)
                if step == "unit" and i < UNITS:
                    hidden_low(i)
                if step == "band":
                    pool.wait_ge(ld_pos, 16)
                    for r in range(TPB):
                        pool.affine_select(out=pos[:, r, :], in_=pos[:, r, :], compare_op=ALU.is_gt, fill=0.0,
                                           base=SPAN + P * r, pattern=[[-1, T]],
                                           channel_multiplier=1).then_inc(band_done, 1)
                    for r in range(TPB):
                        pool.wait_ge(band_done, r + 1)
                        pool.affine_select(out=pos[:, r, :], in_=pos[:, r, :], compare_op=ALU.is_gt, fill=0.0,
                                           base=SPAN - P * r, pattern=[[1, T]],
                                           channel_multiplier=-1).then_inc(band_done, 1)
                if step == "exp":
                    pool.wait_ge(ld_rows, 16)
                    pool.wait_ge(gates_done, 2)
                    pool.tensor_scalar(tgamma[:, :], rows[:, R_GAMMA, :], tx[:, 0:1], None,
                                       ALU.mult).then_inc(pre_done, 1)
                    pool.tensor_scalar(tbeta[:, :], rows[:, R_BETA, :], tx[:, 0:1], None,
                                       ALU.mult).then_inc(pre_done, 1)

        @block.vector
        def _(dve):
            def stats(norm, b, src):
                for i in range(TPB):
                    t = TPB * b + i
                    dve.bn_stats(st[:, norm, t, :], src[:, i, :]).then_inc(st_done[norm], 1)
                for i in range(TPB):
                    t = TPB * b + i
                    dve.wait_ge(st_done[norm], t + 1)
                    dve.bn_aggr(mv[:, norm, t, :], st[:, norm, t, :]).then_inc(mv_done[norm], 1)
                dve.wait_ge(mv_done[norm], TPB * (b + 1))
                dve.tensor_scalar(ve[:, norm, tok(b)], mv[:, norm, tok(b), 1], EPS, None,
                                  ALU.add).then_inc(ve_done[norm], 1)

            def mean(norm, t):
                return mv[:, norm, t, 0:1]

            def inv(norm, t):
                return rstd[:, norm, t:t + 1]

            def ln_x_plus_ctx(b):
                dve.wait_ge(rstd_done[0], b + 1)
                for i in range(TPB):
                    t = TPB * b + i
                    dve.tensor_scalar(emb[:, t, :], x[:, t, :], mean(0, t), inv(0, t),
                                      ALU.subtract, ALU.mult).then_inc(xn_done, 1)
                if b == 0:
                    dve.wait_ge(ld_cx, 16)
                dve.wait_ge(xn_done, TPB * (b + 1))
                dve.tensor_tensor(emb[:, tok(b), :], emb[:, tok(b), :], cx[:, tok(b), :],
                                  ALU.add).then_inc(emb_done, 1)

            def key_max(b):
                dve.wait_ge(kv_ready, b + 1)
                dve.tensor_reduce(kmax[:, b:b + 1], bank[AUX[b]][:, 0:T], AX.X, ALU.max).then_inc(kmax_done, 1)
                dve.wait_ge(kmax_done, b + 1)
                dve.tensor_scalar(kneg[:, b:b + 1], kmax[:, b:b + 1], cols[:, C_BK:C_BK + 1], -1.0,
                                  ALU.add, ALU.mult).then_inc(kneg_done, 1)
                dve.wait_ge(kneg_done, b + 1)
                dve.tensor_scalar(kbias[:, b:b + 1], kneg[:, b:b + 1], cols[:, C_BK:C_BK + 1], None,
                                  ALU.add).then_inc(kbias_done, 1)

            def key_times_value(b):
                dve.wait_ge(ek_done, b + 1)
                dve.scalar_tensor_tensor(out=ekvT[:, b, :], in0=bank[AUX[b]][:, T:2 * T],
                                         scalar=cols[:, C_BV:C_BV + 1], in1=ekT[:, b, :],
                                         op0=ALU.add, op1=ALU.mult).then_inc(ekv_done, 1)

            def aft_out(b):
                dve.wait_ge(aft_ready, b + 1)
                dve.scalar_tensor_tensor(out=y[:, b, :], in0=eq[:, b, :], scalar=1.0, in1=bank[MAIN[b]][:, T:2 * T],
                                         op0=ALU.add, op1=ALU.mult).then_inc(den_done, 1)
                dve.wait_ge(den_done, b + 1)
                for i in range(TPB):
                    cut = slice(P * i, P * i + P)
                    dve.reciprocal(y[:, b, cut], y[:, b, cut]).then_inc(rden_done, 1)
                    dve.wait_ge(rden_done, TPB * b + i + 1)
                    dve.tensor_tensor(y[:, b, cut], y[:, b, cut], bank[MAIN[b]][:, cut], ALU.mult).then_inc(y_done, 1)

            def tiles_in(psum):
                return psum[:, 0:T].rearrange("p (i d) -> p i d", i=TPB)

            def norm1(b):
                dve.wait_ge(rstd_done[1], b + 1)
                for i in range(TPB):
                    t = TPB * b + i
                    dve.tensor_scalar(n1[:, b, i, :], bank[AUX[b]][:, P * i:P * i + P], mean(1, t), inv(1, t),
                                      ALU.subtract, ALU.mult).then_inc(n1_done, 1)

            def centred_z2_times_gamma(b):
                dve.wait_ge(mv_done[2], TPB * (b + 1))
                if b == 0:
                    dve.wait_ge(pre_done, 2)
                for i in range(TPB):
                    t = TPB * b + i
                    dve.scalar_tensor_tensor(out=n2g[:, b, i, :], in0=bank[AUX[b]][:, P * i:P * i + P],
                                             scalar=mean(2, t),
                                             in1=tgamma[:, :], op0=ALU.subtract, op1=ALU.mult).then_inc(n2g_done, 1)

            def gated_x1(b):
                dve.wait_ge(rstd_done[2], b + 1)
                dve.wait_ge(xtb_done, b + 1)
                for i in range(TPB):
                    t = TPB * b + i
                    dve.wait_ge(n2g_done, t + 1)
                    dve.scalar_tensor_tensor(out=x[:, t, :], in0=n2g[:, b, i, :], scalar=inv(2, t),
                                             in1=x[:, t, :], op0=ALU.mult, op1=ALU.add).then_inc(x1_done, 1)
                dve.wait_ge(x1_done, TPB * (b + 1))
                stats(3, b, x[:, tok(b), :])

            def norm3(b):
                dve.wait_ge(rstd_done[3], b + 1)
                for i in range(TPB):
                    t = TPB * b + i
                    dve.tensor_scalar(xf[:, b, i, :], x[:, t, :], mean(3, t), inv(3, t),
                                      ALU.subtract, ALU.mult).then_inc(xf_done, 1)

            def xfT_low(b):
                dve.wait_ge(xfThi_done, b + 1)
                dve.wait_ge(xfT_done, b + 1)
                dve.tensor_tensor(xfT_lo[:, T * b:T * b + T], xfT[:, T * b:T * b + T],
                                  f32(xfT_hi[:, T * b:T * b + T]), ALU.subtract).then_inc(xfTlo_done, 1)

            def pick_top2(h):
                dve.wait_ge(sc_ready, h + 1)
                dve.tensor_copy(sc[:, :, :], bank[SCORE_BANK[h]][:, 0:HT * E].rearrange("p (t e) -> p t e", e=E)) \
                   .then_inc(sc_done, 1)
                dve.wait_ge(sc_done, h + 1)
                for t in range(HT):
                    dve.max(top[:, t, :], sc[:, t, :]).then_inc(top_done, 1)
                for t in range(HT):
                    dve.wait_ge(top_done, HT * h + t + 1)
                    dve.max_index(topi[:, t, :], top[:, t, :], sc[:, t, :]).then_inc(topi_done, 1)
                dve.tensor_tensor(gap[:, :], top[:, :, 0], top[:, :, 1], ALU.subtract).then_inc(gap_done, 1)
                dve.wait_ge(topi_done, HT * (h + 1))
                dve.tensor_copy(topf[:, :, :], topi[:, :, 0:2]).then_inc(topf_done, 1)
                dve.wait_ge(topf_done, h + 1)
                for k in range(2):
                    dve.tensor_tensor(chosen[:, k, :, :],
                                      cols[:, C_IOTA:C_IOTA + E].unsqueeze(1).broadcast_to([P, HT, E]),
                                      topf[:, :, k:k + 1].broadcast_to([P, HT, E]),
                                      ALU.is_equal).then_inc(is_done, 1)

            def route(h):
                dve.wait_ge(tgap_done, h + 1)
                for k, slope in ((0, halftf), (1, neghalftf)):
                    dve.tensor_scalar(pw[:, k, :], tgap[:, :], slope[:, 0:1], halftf[:, 0:1],
                                      ALU.mult, ALU.add).then_inc(pw_done, 1)
                for k in range(2):
                    dve.wait_ge(is_done, 2 * h + k + 1)
                    dve.wait_ge(pw_done, 2 * h + k + 1)
                    dve.tensor_tensor(chosen[:, k, :, :], chosen[:, k, :, :],
                                      pw[:, k, :].unsqueeze(2).broadcast_to([P, HT, E]),
                                      ALU.mult).then_inc(chosen_done, 1)
                dve.wait_ge(chosen_done, 2 * (h + 1))
                dve.tensor_tensor(probs[:, :, :], chosen[:, 0, :, :], chosen[:, 1, :, :],
                                  ALU.add).then_inc(probs_done, 1)

            def copy_pT(h):
                dve.wait_ge(pT_ready, h + 1)
                if h:
                    dve.wait_ge(p_out, 16 * h)
                dve.tensor_copy(pT[:, :], bank[PT_BANK[h]][0:E, :]).then_inc(pT_done, 1)

            def hidden(u):
                dve.wait_ge(silu_done, u + 1)
                dve.wait_ge(h2_ready, u + 1)
                dve.tensor_tensor(hid[:, u % HID_SLOTS, :], hid[:, u % HID_SLOTS, :], bank[H2_BANK[u % 2]][:, :],
                                  ALU.mult).then_inc(hid_done, 1)

            def add_expert(v):
                h, e = divmod(v, E)
                dve.wait_ge(y_ready, ECH * (v + 1))
                dve.wait_ge(p_back[e], 16 * (h + 1))
                dve.tensor_tensor(pall[:, e, :], pall[:, e, :], bank[Y_BANK[v % 2]][:, :],
                                  ALU.mult).then_inc(yp_done, 1)
                if e == 0:
                    dve.wait_ge(x1T_done, 2 * (h + 1))
                dve.wait_ge(yp_done, v + 1)
                if v:
                    dve.wait_ge(acc_done, v)
                dve.tensor_tensor(acc[:, HALF * h:HALF * h + HALF], acc[:, HALF * h:HALF * h + HALF],
                                  pall[:, e, :], ALU.add).then_inc(acc_done, 1)

            for step, i in STEPS:
                if step == "x stats":
                    dve.wait_ge(ld_x[i], 16)
                    stats(0, i, x[:, tok(i), :])
                if step == "emb":
                    ln_x_plus_ctx(i)
                if step == "key maximum":
                    key_max(i)
                if step == "ek and ekv":
                    key_times_value(i)
                if step == "aft":
                    aft_out(i)
                if step == "z1":
                    dve.wait_ge(z1_ready, i + 1)
                    stats(1, i, tiles_in(bank[AUX[i]]))
                if step == "a":
                    norm1(i)
                if step == "z2":
                    dve.wait_ge(z2_ready, i + 1)
                    stats(2, i, tiles_in(bank[AUX[i]]))
                if step == "z2 times gamma":
                    centred_z2_times_gamma(i)
                if step == "x1":
                    gated_x1(i)
                if step == "xf":
                    norm3(i)
                if step == "xf low":
                    xfT_low(i)
                if step == "scores":
                    pick_top2(i)
                if step == "route":
                    route(i)
                if step == "probs":
                    copy_pT(i)
                if step == "unit":
                    if i < UNITS:
                        hidden(i)
                    if i >= ADD_LAG and i % ECH == 0:
                        add_expert((i - ADD_LAG) // ECH)
                if step == "exp":
                    for r in range(TPB):
                        dve.wait_ge(band_done, TPB + r + 1)
                        dve.tensor_reduce(wmax[:, r:r + 1], pos[:, r, :], AX.X, ALU.max).then_inc(wmax_done, 1)
                    dve.wait_ge(wmax_done, TPB)
                    dve.tensor_scalar(wneg[:, :], wmax[:, :], -1.0, None, ALU.mult).then_inc(wneg_done, 1)
                    dve.wait_ge(ld_cols, 16)
                    dve.tensor_scalar(negbq[:, :], cols[:, C_BQ:C_BQ + 1], -1.0, None, ALU.mult).then_inc(consts_done, 1)
                    dve.tensor_tensor(betab2[:, :], cols[:, C_BETA:C_BETA + 1], cols[:, C_B2:C_B2 + 1],
                                      ALU.add).then_inc(b2_done, 1)
                    dve.wait_ge(gates_done, 2)
                    dve.tensor_scalar(halftf[:, :], tf[:, :], 0.5, None, ALU.mult).then_inc(consts_done, 1)
                    dve.tensor_scalar(neghalftf[:, :], tf[:, :], -0.5, None, ALU.mult).then_inc(consts_done, 1)

        @block.scalar
        def _(act):
            act.dma_start(ident[:, :], ident_in).then_inc(ld_ident, 16)
            act.dma_start(cols[:, :], cols_in).then_inc(ld_cols, 16)
            act.dma_start(pos[:, :, :], pos_in).then_inc(ld_pos, 16)
            act.dma_start(rows[:, :, :], rows_in).then_inc(ld_rows, 16)
            act.dma_start(gate[:, :], gate_in).then_inc(ld_gate, 16)

            def copy(dst, src):
                return act.activation(dst, src, ACT.Copy)

            def split_high(e):
                act.wait_ge(ld_raw[e % RAW_SLOTS], 16 * (e // RAW_SLOTS + 1))
                copy(ex_hi[:, e, :], raw[:, e % RAW_SLOTS, :]).then_inc(whi_done, 1)

            def copy_embT(b):
                act.wait_ge(embT_ready, b + 1)
                copy(embT[:, b, :], bank[MAIN[b]][:, 0:T]).then_inc(embT_done, 1)

            def exp_key(b):
                act.wait_ge(kbias_done, b + 1)
                act.activation(ekT[:, b, :], bank[AUX[b]][:, 0:T], ACT.Exp,
                               bias=kbias[:, b:b + 1]).then_inc(ek_done, 1)

            def exp_query(b):
                if b == 0:
                    act.wait_ge(consts_done, 1)
                act.wait_ge(q_ready, b + 1)
                act.activation(eq[:, b, :], bank[MAIN[b]][:, 0:T], ACT.Exp, bias=negbq[:, 0:1],
                               scale=-1.0).then_inc(eq_done, 1)

            def copy_kv(b):
                act.wait_ge(kvT_ready, b + 1)
                copy(kv[:, b, :, :, :].rearrange("p i k d -> p (i k d)"),
                     bank[AUX[b]][:, :]).then_inc(kv_done, 1)

            def a_transposed(b):
                if b == 0:
                    act.wait_ge(b2_done, 1)
                act.wait_ge(n1T_ready, b + 1)
                for dst, bias, done in ((aT, cols[:, C_BETA:C_BETA + 1], aT_done), (aTb, betab2[:, 0:1], aTb_done)):
                    act.activation(dst[:, b, :], bank[MAIN[b]][:, T:2 * T], ACT.Identity, bias=bias,
                                   scale=cols[:, C_GAMMA:C_GAMMA + 1]).then_inc(done, 1)

            def relu(b, s):
                act.wait_ge(ff1_ready[b], s + 1)
                for c in range(2):
                    act.activation(hr[:, b, 2 * s + c, :], bank[[AUX, MAIN][s][b]][:, T * c:T * c + T], ACT.Relu,
                                   bias=cols[:, C_B1 + 2 * s + c:C_B1 + 2 * s + c + 1]).then_inc(hr_done[b], 1)

            def xfT_high(b):
                act.wait_ge(xfT_ready, b + 1)
                copy(xfT_hi[:, T * b:T * b + T], bank[MAIN[b]][:, 0:T]).then_inc(xfThi_done, 1)
                copy(xfT[:, T * b:T * b + T], bank[MAIN[b]][:, 0:T]).then_inc(xfT_done, 1)
                copy(acc[:, T * b:T * b + T], bank[AUX[b]][:, T:2 * T]).then_inc(x1T_done, 1)

            def silu(u):
                act.wait_ge(h1_ready, u + 1)
                if u >= HID_SLOTS:
                    act.wait_ge(hidlo_done, u - HID_SLOTS + 1)
                act.activation(hid[:, u % HID_SLOTS, :], bank[H1_BANK[u % 2]][:, :], ACT.Silu).then_inc(silu_done, 1)

            def hidden_high(u):
                act.wait_ge(hid_done, u + 1)
                if u >= HID_SLOTS:
                    act.wait_ge(y_ready, u - HID_SLOTS + 1)
                copy(hid_hi[:, u % HID_SLOTS, :], hid[:, u % HID_SLOTS, :]).then_inc(hidhi_done, 1)

            for step, i in STEPS:
                if step == "keys and values":
                    copy_embT(i)
                if step == "key maximum":
                    exp_key(i)
                if step == "query":
                    exp_query(i)
                if step == "ek and ekv":
                    copy_kv(i)
                if step == "a":
                    a_transposed(i)
                if step == "feed forward 0":
                    relu(i, 0)
                if step == "feed forward 1":
                    relu(i, 1)
                if step == "xf":
                    xfT_high(i)
                if step == "scores":
                    act.wait_ge(gap_done, i + 1)
                    act.activation(tgap[:, :], gap[:, :], ACT.Tanh, scale=0.5).then_inc(tgap_done, 1)
                if step == "split high":
                    split_high(i)
                if step == "unit":
                    if i < UNITS:
                        silu(i)
                    if 0 < i <= UNITS:
                        hidden_high(i - 1)
                if step == "band":
                    act.wait_ge(ld_cols, 16)
                    act.activation(tx[:, :], cols[:, C_GX:C_GX + 1], ACT.Tanh).then_inc(gates_done, 1)
                    act.activation(tf[:, :], cols[:, C_GF:C_GF + 1], ACT.Tanh).then_inc(gates_done, 1)
                if step == "exp":
                    act.wait_ge(wneg_done, 1)
                    for r in range(TPB):
                        act.activation(pos[:, r, :], pos[:, r, :], ACT.Exp, bias=wneg[:, r:r + 1]).then_inc(ew_done, 1)
                if step == "transposed":
                    act.wait_ge(ewT_ready, 1)
                    copy(ewT[:, :, :].rearrange("p i t -> p (i t)"), bank[EW_BANK][:, :]).then_inc(ewT_done, 1)
            act.wait_ge(acc_done, E)
            act.dma_start(out[:, 0:HALF], acc[:, 0:HALF]).then_inc(out_done, 16)

        @block.tensor
        def _(pe):
            def product(dst, w_hi, w_lo, m_hi, m_lo, first=True, last=True):
                pe.matmul(dst, w_hi, m_hi, start=first, stop=False)
                pe.matmul(dst, w_hi, m_lo, start=False, stop=False)
                return pe.matmul(dst, w_lo, m_hi, start=False, stop=last)

            def transpose_emb(b):
                pe.wait_ge(emb_done, b + 1)
                for i in range(TPB):
                    mm = pe.transpose(bank[MAIN[b]][:, P * i:P * i + P], emb[:, TPB * b + i, :], ident[:, :])
                mm.then_inc(embT_ready, 1)

            def project(dst, w, b):
                return pe.matmul(dst, wa[:, w, :], embT[:, b, :], start=True, stop=True)

            def keys_values(b):
                if b == 0:
                    pe.wait_ge(ld_wa, 16)
                pe.wait_ge(embT_done, b + 1)
                project(bank[AUX[b]][:, 0:T], WK, b)
                project(bank[AUX[b]][:, T:2 * T], WV, b).then_inc(kv_ready, 1)

            def queries(b):
                if AUX[b] == MAIN[b]:
                    pe.wait_ge(ekv_done, b + 1)
                project(bank[MAIN[b]][:, 0:T], WQ, b).then_inc(q_ready, 1)

            def kvT(b):
                pe.wait_ge(ekv_done, b + 1)
                if AUX[b] == MAIN[b]:
                    pe.wait_ge(eq_done, b + 1)
                for i in range(TPB):
                    for k, src in enumerate((ekvT, ekT)):
                        mm = pe.transpose(bank[AUX[b]][:, P * (2 * i + k):P * (2 * i + k + 1)],
                                          src[:, b, P * i:P * i + P], ident[:, :])
                mm.then_inc(kvT_ready, 1)

            def aft(b):
                if b == 0:
                    pe.wait_ge(ewT_done, 1)
                pe.wait_ge(kv_done, b + 1)
                pe.wait_ge(eq_done, b + 1)
                for k in (1, 0):
                    for i in range(TPB):
                        mm = pe.matmul(bank[MAIN[b]][:, T * k:T * k + T], kv[:, b, i, k, :], ewT[:, i, :],
                                       start=(i == 0), stop=(i == TPB - 1))
                mm.then_inc(aft_ready, 1)

            def z1(b):
                if AUX[b] == MAIN[b]:
                    pe.wait_ge(y_done, TPB * (b + 1))
                pe.wait_ge(embb_done, b + 1)
                for i in range(TPB):
                    psum = bank[AUX[b]][:, P * i:P * i + P]
                    pe.matmul(psum, ident[:, :], emb[:, TPB * b + i, :], start=True, stop=False)
                    pe.wait_ge(y_done, TPB * b + i + 1)
                    mm = pe.matmul(psum, y[:, b, P * i:P * i + P], wa[:, WO, :], start=False, stop=True)
                mm.then_inc(z1_ready, 1)

            def n1T(b):
                pe.wait_ge(n1_done, TPB * (b + 1))
                for i in range(TPB):
                    mm = pe.transpose(bank[MAIN[b]][:, T + P * i:T + P * i + P], n1[:, b, i, :], ident[:, :])
                mm.then_inc(n1T_ready, 1)

            def ff1(b, s):
                if s == 0:
                    if b == 0:
                        pe.wait_ge(ld_w1, 16)
                    pe.wait_ge(aT_done, b + 1)
                    if AUX[b] == MAIN[b]:
                        pe.wait_ge(aTb_done, b + 1)
                elif AUX[b] == MAIN[b]:
                    pe.wait_ge(hr_done[b], HCH // 2)
                else:
                    pe.wait_ge(aTb_done, b + 1)
                for c in range(2):
                    cut = slice(P * (2 * s + c), P * (2 * s + c) + P)
                    mm = pe.matmul(bank[[AUX, MAIN][s][b]][:, T * c:T * c + T], w1[:, cut], aT[:, b, :],
                                   start=True, stop=True)
                mm.then_inc(ff1_ready[b], 1)

            def z2(b):
                if b == 0:
                    pe.wait_ge(ld_w2, 16)
                psum = bank[AUX[b]]
                for i in range(TPB):
                    for c in range(HCH):
                        if c == 0:
                            pe.wait_ge(hr_done[b], HCH if AUX[b] == MAIN[b] else HCH // 2)
                            pe.matmul(psum[:, P * i:P * i + P], aTb[:, b, P * i:P * i + P], ident[:, :],
                                      start=True, stop=False)
                        if c == HCH // 2:
                            pe.wait_ge(hr_done[b], HCH)
                        mm = pe.matmul(psum[:, P * i:P * i + P], hr[:, b, c, P * i:P * i + P], w2[:, c, :],
                                       start=False, stop=(c == HCH - 1))
                mm.then_inc(z2_ready, 1)

            def xf_x1_T(b):
                pe.wait_ge(xf_done, TPB * (b + 1))
                for i in range(TPB):
                    pe.transpose(bank[AUX[b]][:, T + P * i:T + P * i + P], x[:, TPB * b + i, :], ident[:, :])
                for i in range(TPB):
                    mm = pe.transpose(bank[MAIN[b]][:, P * i:P * i + P], xf[:, b, i, :], ident[:, :])
                mm.then_inc(xfT_ready, 1)

            def scores(h):
                if h == 0:
                    pe.wait_ge(ld_gate, 16)
                pe.wait_ge(xfT_done, 2 * (h + 1))
                if SCORE_BANK[h] in MAIN:
                    pe.wait_ge(x1T_done, 2 * (h + 1))
                for t in range(HT):
                    cut = slice(HALF * h + P * t, HALF * h + P * t + P)
                    mm = pe.matmul(bank[SCORE_BANK[h]][:, E * t:E * t + E], xfT[:, cut], gate[:, :],
                                   start=True, stop=True)
                mm.then_inc(sc_ready, 1)

            def probsT(h):
                pe.wait_ge(probs_done, h + 1)
                for t in range(HT):
                    mm = pe.transpose(bank[PT_BANK[h]][0:E, P * t:P * t + P], probs[:, t, :], ident[:, :])
                mm.then_inc(pT_ready, 1)

            def expert_in(u):
                h, e, c = u // UPH, u % UPH // ECH, u % ECH
                pe.wait_ge(wlo_done, e + 1)
                pe.wait_ge(xfTlo_done, 2 * (h + 1))
                pe.wait_ge(x1T_done, 2 * (h + 1))
                tokens = slice(HALF * h, HALF * h + HALF)
                for part, (banks, freed, ready) in enumerate(((H1_BANK, silu_done, h1_ready),
                                                              (H2_BANK, hid_done, h2_ready))):
                    if u >= 2:
                        pe.wait_ge(freed, u - 1)
                    cut = slice(EH * part + P * c, EH * part + P * c + P)
                    product(bank[banks[u % 2]][:, :], ex_hi[:, e, cut], ex_lo[:, e, cut],
                            xfT_hi[:, tokens], xfT_lo[:, tokens]).then_inc(ready, 1)

            def expert_out(u):
                e, c, v = u % UPH // ECH, u % ECH, u // ECH
                pe.wait_ge(hidlo_done, u + 1)
                if v == 1:
                    pe.wait_ge(pT_done, 1)
                if v >= 2 and c == 0:
                    pe.wait_ge(yp_done, v - 1)
                cut = slice(2 * EH + D * c, 2 * EH + D * c + D)
                product(bank[Y_BANK[v % 2]][:, :], ex_hi[:, e, cut], ex_lo[:, e, cut],
                        hid_hi[:, u % HID_SLOTS, :], hid_lo[:, u % HID_SLOTS, :],
                        first=(c == 0), last=(c == ECH - 1)).then_inc(y_ready, 1)

            pe.wait_ge(ld_ident, 16)
            for step, i in STEPS:
                if step == "emb":
                    transpose_emb(i)
                if step == "keys and values":
                    keys_values(i)
                if step == "query":
                    queries(i)
                if step == "ek and ekv":
                    kvT(i)
                if step == "aft":
                    aft(i)
                if step == "z1":
                    z1(i)
                if step == "a":
                    n1T(i)
                if step == "feed forward 0":
                    ff1(i, 0)
                if step == "feed forward 1":
                    ff1(i, 1)
                if step == "z2":
                    z2(i)
                if step == "xf":
                    xf_x1_T(i)
                if step == "scores":
                    scores(i)
                if step == "probs":
                    probsT(i)
                if step == "unit":
                    if i < UNITS:
                        expert_in(i)
                    if OUT_LAG <= i < UNITS + OUT_LAG:
                        expert_out(i - OUT_LAG)
                if step == "exp":
                    pe.wait_ge(ew_done, TPB)
                    for k in range(TPB):
                        for r in range(TPB):
                            mm = pe.transpose(bank[EW_BANK][:, T * k + P * r:T * k + P * r + P],
                                              pos[:, r, P * k:P * k + P], ident[:, :])
                    mm.then_inc(ewT_ready, 1)


def kernel(**inputs):
    import numpy as np
    import concourse.bacc as bacc
    from concourse import mybir as mb
    from concourse.bass_utils import run_bass_kernel_spmd

    g = {k: np.asarray(v) for k, v in inputs.items()}
    a = {k[len("L0_xattn_"):]: v for k, v in g.items() if k.startswith("L0_xattn_")}
    f = {k[len("L0_ffn_"):]: v for k, v in g.items() if k.startswith("L0_ffn_")}

    def token_rows(v):
        return v.reshape(TILES, P, D).transpose(1, 0, 2)

    def on_partitions(v):
        return v.reshape(-1, P).T

    iota = np.tile(np.arange(E, dtype=np.float32), (P, 1))
    cols = np.concatenate([on_partitions(a[n]) for n in ("bq", "bk", "bv", "bo", "gamma", "beta", "b2", "b1")]
                          + [np.tile(g[n].reshape(1, 1), (P, 1)) for n in ("g_xattn", "g_ffn")] + [iota], axis=1)
    rows = np.stack([np.tile(a[n], (P, 1)) for n in ("gamma", "beta", "bo")], axis=1)
    experts = np.concatenate([f["w12"].transpose(2, 0, 1),
                              f["w3"].reshape(E, D, ECH, P).transpose(3, 0, 2, 1).reshape(P, E, ECH * D)], axis=2)
    feeds = {
        "x_in": token_rows(g["x"]),
        "ctx_in": token_rows(g["ctx_1024"]),
        "ident_in": np.eye(P, dtype=np.float32),
        "cols_in": cols,
        "rows_in": rows,
        "pos_in": a["pos_bias"].reshape(TPB, P, T).transpose(1, 0, 2),
        "wa_in": np.stack([a[n] for n in ("wq", "wk", "wv", "wo")], axis=1),
        "w1_in": a["w1"],
        "w2_in": a["w2"].reshape(HCH, P, D).transpose(1, 0, 2),
        "gate_in": f["gate_w"].T,
        "experts_in": experts,
    }
    nc = bacc.Bacc("TRN2", target_bir_lowering=False, num_devices=1)
    feeds = {k: np.ascontiguousarray(v) for k, v in feeds.items()}
    aps = [nc.dram_tensor(k, v.shape, mb.dt.from_np(v.dtype), kind="ExternalInput").ap() for k, v in feeds.items()]
    out = nc.dram_tensor("out", (P, N), mb.dt.float32, kind="ExternalOutput").ap()
    build(nc, *aps, out)
    done = run_bass_kernel_spmd(nc, [feeds], core_ids=[0])
    return done.results[0]["out"].T.reshape(B, T, D)
```

```python
from contextlib import ExitStack

import concourse.bass as bass
from concourse import mybir
from concourse.alu_op_type import AluOpType as ALU

F32 = mybir.dt.float32
F32R = mybir.dt.float32r
U32 = mybir.dt.uint32
ACT = mybir.ActivationFunctionType
AX = mybir.AxisListType

P = 128
B, T, D = 4, 256, 128
N = B * T
TILES = N // P
TPB = T // P
HID = 512
HCH = HID // P
E = 8
EH = 256
ECH = EH // P
SPAN = 32
EPS = 1e-5
HALVES = 2
HALF = N // HALVES
HT = TILES // HALVES
UPH = E * ECH
UNITS = HALVES * UPH

STEP_AT = {
    "x stats": (0, 1, 11, 17),
    "emb": (2, 5, 19, 27),
    "emb transposed": (4, 6, 24, 35),
    "keys and values": (7, 8, 30, 40),
    "key maximum": (10, 16, 31, 50),
    "query": (12, 21, 46, 58),
    "emb + bo": (37, 42, 45, 72),
    "x + beta": (38, 44, 57, 85),
    "ekv": (13, 25, 33, 55),
    "ek and ekv transposed": (15, 29, 48, 62),
    "aft": (22, 32, 52, 66),
    "y": (28, 49, 68, 70),
    "attention": (39, 51, 75, 81),
    "z1 stats": (54, 60, 76, 82),
    "n1": (59, 69, 78, 89),
    "a": (65, 77, 86, 92),
    "a + b2": (61, 73, 90, 112),
    "feed forward 0": (71, 83, 95, 99),
    "feed forward 1": (74, 84, 100, 108),
    "feed forward 2": (79, 91, 105, 115),
    "z2 stats": (87, 94, 109, 122),
    "z2 times gamma": (88, 97, 116, 132),
    "x1": (93, 102, 120, 139),
    "xf": (96, 104, 138, 151),
    "xf transposed": (101, 107, 152, 166),
    "xf low": (106, 114, 163, 168),
    "scores": (111, 174),
    "top 2": (118, 188),
    "route": (134, 193),
    "probs transposed": (140, 215),
}
WEIGHTS_AT = {"band": 3, "exp": 9, "ew": 14}
HI_AT = [18, 23, 26, 41, 64, 67, 113, 124]
LO_AT = [20, 34, 36, 43, 47, 53, 56, 63, 80, 98, 103, 110, 117, 129, 133, 172]
IN_AT = ([119, 121, 127, 128, 141, 144, 148, 155, 157, 167, 177, 179, 181, 183, 192, 198]
         + [205, 207, 209, 213, 222, 227, 230, 231, 235, 238, 242, 246, 251, 264, 268, 270])
HID_AT = ([123, 125, 135, 136, 142, 145, 150, 158, 162, 176, 178, 182, 187, 189, 200, 201]
          + [208, 211, 218, 219, 225, 229, 233, 237, 240, 244, 248, 254, 262, 265, 273, 274])
SPLIT_AT = ([126, 130, 137, 143, 147, 149, 160, 165, 169, 180, 185, 186, 195, 196, 203, 206]
            + [214, 217, 224, 226, 234, 236, 245, 247, 253, 257, 259, 260, 269, 272, 276, 278])
OUT_AT = ([131, 146, 154, 156, 159, 164, 171, 173, 184, 190, 191, 197, 199, 202, 210, 216]
          + [221, 223, 228, 232, 241, 249, 250, 252, 256, 261, 266, 267, 275, 277, 279, 281])
SUM_AT = [153, 161, 170, 175, 194, 204, 212, 220, 239, 243, 255, 258, 263, 271, 280, 282]
HID_SLOTS = 4
WARM_UPS = 5


def steps():
    timed = [(at, name, i) for name, ats in STEP_AT.items() for i, at in enumerate(ats)]
    timed += [(at, name, None) for name, at in WEIGHTS_AT.items()]
    for name, ats in (("weights high", HI_AT), ("weights low", LO_AT), ("unit in", IN_AT), ("hidden", HID_AT),
                      ("hidden split", SPLIT_AT), ("unit out", OUT_AT), ("expert sum", SUM_AT)):
        timed += [(at, name, i) for i, at in enumerate(ats)]
    return [(name, i) for _, name, i in sorted(timed, key=lambda t: t[0])]


STEPS = steps()

MAIN = [0, 2, 4, 5]
AUX = [1, 3, 4, 5]
H1_BANK, H2_BANK, Y_BANK = [0, 1], [2, 3], [6, 7]
EW_BANK = 7
SCORE_BANK, PT_BANK = [7, 4], [7, 5]

C_BQ, C_BK, C_BV, C_GAMMA, C_BETA, C_B1 = 0, 1, 2, 3, 4, 5
C_GX = C_B1 + HCH
C_GF, C_IOTA = C_GX + 1, C_GX + 2
N_COLS = C_IOTA + E
R_GAMMA, R_BETA, R_BO, R_B2, N_ROWS = 0, 1, 2, 3, 4
WQ, WK, WV, WO = 0, 1, 2, 3

RAW_SLOTS = 4
EXPERT_COLS = 2 * EH + ECH * D


def build(nc, x_in, ctx_in, ident_in, cols_in, rows_in, pos_in, wa_in, w1_in, w2_in, gate_in, experts_in, out):
    with ExitStack() as stack:
        def sb(name, shape, dt=F32):
            return stack.enter_context(nc.sbuf_tensor(name, shape, dt))

        def sem(name):
            return stack.enter_context(nc.semaphore(name))

        x = sb("x", [P, TILES, D])
        cx = sb("cx", [P, TILES, D])
        ident = sb("ident", [P, P])
        cols = sb("cols", [P, N_COLS])
        rows = sb("rows", [P, N_ROWS, D])
        pos = sb("pos", [P, TPB, T])
        gate = sb("gate", [P, E])
        raw = sb("raw", [P, RAW_SLOTS, EXPERT_COLS])

        wa, w1, w2 = sb("wa", [P, 4, D]), sb("w1", [P, HID]), sb("w2", [P, HCH, D])
        ewT = sb("ewT", [P, TPB, T])
        ex_hi, ex_lo = sb("ex_hi", [P, E, EXPERT_COLS], F32R), sb("ex_lo", [P, E, EXPERT_COLS], F32R)

        wmax, wneg = sb("wmax", [P, TPB]), sb("wneg", [P, TPB])
        st = sb("st", [P, 4, TILES, 6])
        mv = sb("mv", [P, 4, TILES, 2])
        ve = sb("ve", [P, 4, TILES])
        rstd, shift = sb("rstd", [P, 4, TILES]), sb("shift", [P, 4, TILES])
        mhalf = sb("mhalf", [P, TPB])
        kmax, kneg, kbias = sb("kmax", [P, B]), sb("kneg", [P, B]), sb("kbias", [P, B])
        negbq = sb("negbq", [P, 1])
        tx, tf = sb("tx", [P, 1]), sb("tf", [P, 1])
        halftf, neghalftf = sb("halftf", [P, 1]), sb("neghalftf", [P, 1])
        tgamma, tbeta = sb("tgamma", [P, D]), sb("tbeta", [P, D])

        emb = sb("emb", [P, TILES, D])
        embT = sb("embT", [P, B, T])
        ekT, ekvT, eq = sb("ekT", [P, B, T]), sb("ekvT", [P, B, T]), sb("eq", [P, B, T])
        kv = sb("kv", [P, B, TPB, 2, D])
        y = sb("y", [P, B, T])
        n1 = sb("n1", [P, B, TPB, D])
        aT = sb("aT", [P, B, T])
        ab = sb("ab", [P, B, TPB, D])
        hr = sb("hr", [P, B, HCH, T])
        xf = sb("xf", [P, B, TPB, D])
        xfT = sb("xfT", [P, N])
        xfT_hi, xfT_lo = sb("xfT_hi", [P, N], F32R), sb("xfT_lo", [P, N], F32R)

        sc = sb("sc", [P, HT, E])
        top = sb("top", [P, HT, 8])
        topi = sb("topi", [P, HT, 8], U32)
        topf = sb("topf", [P, HT, 2])
        gap, tgap = sb("gap", [P, HT]), sb("tgap", [P, HT])
        pw = sb("pw", [P, 2, HT])
        chosen = sb("chosen", [P, 2, HT, E])
        probs = sb("probs", [P, HT, E])
        pT = sb("pT", [E, HALF])
        pall = sb("pall", [P, E, HALF])
        p_dram = nc.dram_tensor("p_dram", (HALVES, E, HALF), F32, kind="Internal").ap()

        zeros = sb("zeros", [P, T])

        hid = sb("hid", [P, HID_SLOTS, HALF])
        hid_hi, hid_lo = sb("hid_hi", [P, HID_SLOTS, HALF], F32R), sb("hid_lo", [P, HID_SLOTS, HALF], F32R)
        acc = sb("acc", [P, N])

        bank = [stack.enter_context(nc.psum_tensor(f"bank{i}", [P, 512], F32)) for i in range(8)]

        ld_x = [sem(f"ld_x{b}") for b in range(B)]
        ld_cx = [sem(f"ld_cx{h}") for h in range(HALVES)]
        ld_ident, ld_cols, ld_rows = sem("ld_ident"), sem("ld_cols"), sem("ld_rows")
        ld_pos, ld_gate, ld_wa, ld_w1, ld_w2 = sem("ld_pos"), sem("ld_gate"), sem("ld_wa"), sem("ld_w1"), sem("ld_w2")
        ld_raw = [sem(f"ld_raw{s}") for s in range(RAW_SLOTS)]
        p_out, out_done = sem("p_out"), sem("out_done")
        p_back = [sem(f"p_back{e}") for e in range(E)]
        half_set, band_done, pre_done, wlo_done = sem("half_set"), sem("band_done"), sem("pre_done"), sem("wlo_done")
        rstd_done = [sem(f"rstd{k}_done") for k in range(4)]
        shift_done = [sem(f"shift{k}_done") for k in range(4)]
        hidlo_done, xtb_done, embb_done = sem("hidlo_done"), sem("xtb_done"), sem("embb_done")
        consts_done, zeros_done = sem("consts_done"), sem("zeros_done")
        wmax_done, wneg_done = sem("wmax_done"), sem("wneg_done")
        st_done = [sem(f"st{k}_done") for k in range(4)]
        mv_done = [sem(f"mv{k}_done") for k in range(4)]
        ve_done = [sem(f"ve{k}_done") for k in range(4)]
        xn_done, emb_done = sem("xn_done"), sem("emb_done")
        kmax_done, kneg_done, kbias_done, ekv_done = sem("kmax_done"), sem("kneg_done"), sem("kbias_done"), sem("ekv_done")
        den_done, rden_done, y_done = sem("den_done"), sem("rden_done"), sem("y_done")
        n1_done = sem("n1_done")
        n2g_done, x1_done = sem("n2g_done"), sem("x1_done")
        xf_done, xfTlo_done = sem("xf_done"), sem("xfTlo_done")
        sc_done, top_done, topi_done, topf_done = sem("sc_done"), sem("top_done"), sem("topi_done"), sem("topf_done")
        gap_done, pw_done, is_done, chosen_done = sem("gap_done"), sem("pw_done"), sem("is_done"), sem("chosen_done")
        probs_done, pT_done = sem("probs_done"), sem("pT_done")
        last_lo_done = sem("last_lo_done")
        hid_done, yp_done, acc_done = sem("hid_done"), sem("yp_done"), sem("acc_done")
        gates_done, ew_done, ewT_done, whi_done = sem("gates_done"), sem("ew_done"), sem("ewT_done"), sem("whi_done")
        embT_done, ek_done, eq_done, kv_done = sem("embT_done"), sem("ek_done"), sem("eq_done"), sem("kv_done")
        aT_done = sem("aT_done")
        hr_done, ff1_ready = [sem(f"hr{b}_done") for b in range(B)], [sem(f"ff1_{b}_ready") for b in range(B)]
        xfT_done, xfThi_done, x1T_done, tgap_done = sem("xfT_done"), sem("xfThi_done"), sem("x1T_done"), sem("tgap_done")
        silu_done, hidhi_done = sem("silu_done"), sem("hidhi_done")
        ewT_ready, embT_ready, kv_ready, q_ready = sem("ewT_ready"), sem("embT_ready"), sem("kv_ready"), sem("q_ready")
        kvT_ready, aft_ready, attn_ready = sem("kvT_ready"), sem("aft_ready"), sem("attn_ready")
        z1_done, z2_done, ag_done, ab_done = sem("z1_done"), sem("z2_done"), sem("ag_done"), sem("ab_done")
        n1T_ready, ff2_ready = sem("n1T_ready"), sem("ff2_ready")
        xfT_ready = sem("xfT_ready")
        sc_ready, pT_ready = sem("sc_ready"), sem("pT_ready")
        h1_ready, h2_ready, y_ready = sem("h1_ready"), sem("h2_ready"), sem("y_ready")

        def parts(u):
            return (slice(0, T), slice(T, HALF)) if u == UNITS - 1 else (slice(0, HALF),)

        def y_bank(v, part):
            return bank[H1_BANK[(UNITS - ECH) % 2] if part else Y_BANK[v % 2]]

        def tok(b):
            return slice(TPB * b, TPB * b + TPB)

        def f32(ap):
            return ap.bitcast(F32)

        block = stack.enter_context(nc.Block())

        @block.sync
        def _(sp):
            sp.dma_start(x[:, tok(0), :], x_in[:, tok(0), :]).then_inc(ld_x[0], 16)
            sp.dma_start(x[:, tok(1), :], x_in[:, tok(1), :]).then_inc(ld_x[1], 16)
            sp.dma_start(cx[:, 0:HT, :], ctx_in[:, 0:HT, :]).then_inc(ld_cx[0], 16)
            sp.dma_start(wa[:, :, :], wa_in).then_inc(ld_wa, 16)
            for b in (2, 3):
                sp.dma_start(x[:, tok(b), :], x_in[:, tok(b), :]).then_inc(ld_x[b], 16)
            sp.dma_start(cx[:, HT:TILES, :], ctx_in[:, HT:TILES, :]).then_inc(ld_cx[1], 16)
            sp.dma_start(w1[:, :], w1_in).then_inc(ld_w1, 16)
            sp.dma_start(w2[:, :, :], w2_in).then_inc(ld_w2, 16)
            for e in range(E):
                if e >= RAW_SLOTS:
                    sp.wait_ge(wlo_done, 2 * (e - RAW_SLOTS + 1))
                sp.dma_start(raw[:, e % RAW_SLOTS, :], experts_in[:, e, :]).then_inc(ld_raw[e % RAW_SLOTS], 16)
            for h in range(HALVES):
                sp.wait_ge(pT_done, h + 1)
                sp.dma_start(p_dram[h], pT[:, :]).then_inc(p_out, 16)
                sp.wait_ge(p_out, 16 * (h + 1))
                for e in range(E):
                    if h:
                        sp.wait_ge(acc_done, e + 1)
                    sp.dma_start(pall[:, e, :], p_dram[h, e, :].partition_broadcast(P)).then_inc(p_back[e], 16)
            sp.wait_ge(acc_done, E * HALVES)
            sp.dma_start(out[:, HALF:HALF + T], acc[:, HALF:HALF + T]).then_inc(out_done, 16)
            sp.wait_ge(acc_done, E * HALVES + 1)
            sp.dma_start(out[:, HALF + T:N], acc[:, HALF + T:N]).then_inc(out_done, 16)
            sp.wait_ge(out_done, 16 * 3)

        @block.gpsimd
        def _(pool):
            def inv_std(norm, b):
                pool.wait_ge(ve_done[norm], b + 1)
                pool.tensor_tensor(rstd[:, norm, tok(b)], ve[:, norm, tok(b)], mhalf[:, :],
                                   ALU.pow).then_inc(rstd_done[norm], 1)

            def split_low(e, part):
                cut = (slice(0, 2 * EH), slice(2 * EH, EXPERT_COLS))[part]
                pool.wait_ge(whi_done, e + 1)
                pool.tensor_tensor(ex_lo[:, e, cut], raw[:, e % RAW_SLOTS, cut], f32(ex_hi[:, e, cut]),
                                   ALU.subtract).then_inc(wlo_done, 1)

            def x_with_beta(b):
                pool.wait_ge(pre_done, 2)
                pool.wait_ge(xn_done, TPB * (b + 1))
                pool.tensor_tensor(x[:, tok(b), :], x[:, tok(b), :],
                                   tbeta[:, :].unsqueeze(1).broadcast_to([P, TPB, D]),
                                   ALU.add).then_inc(xtb_done, 1)

            def emb_plus_bo(b):
                pool.wait_ge(embT_ready, b + 1)
                pool.tensor_tensor(emb[:, tok(b), :], emb[:, tok(b), :],
                                   rows[:, R_BO, :].unsqueeze(1).broadcast_to([P, TPB, D]),
                                   ALU.add).then_inc(embb_done, 1)

            def a_plus_b2(b):
                pool.wait_ge(n1_done, TPB * (b + 1))
                pool.tensor_tensor(ab[:, b, :, :], n1[:, b, :, :],
                                   rows[:, R_GAMMA, :].unsqueeze(1).broadcast_to([P, TPB, D]),
                                   ALU.mult).then_inc(ag_done, 1)
                pool.wait_ge(ag_done, b + 1)
                pool.wait_ge(pre_done, 3)
                pool.tensor_tensor(ab[:, b, :, :], ab[:, b, :, :],
                                   rows[:, R_B2, :].unsqueeze(1).broadcast_to([P, TPB, D]),
                                   ALU.add).then_inc(ab_done, 1)

            def hidden_low(u):
                pool.wait_ge(hidhi_done, u + 1)
                s = u % HID_SLOTS
                if u >= HID_SLOTS:
                    pool.wait_ge(y_ready, u - HID_SLOTS + 1)
                pool.tensor_tensor(hid_lo[:, s, :], hid[:, s, :], f32(hid_hi[:, s, :]),
                                   ALU.subtract).then_inc(hidlo_done, 1)

            pool.memset(mhalf[:, :], -0.5).then_inc(half_set, 1)
            pool.wait_ge(half_set, 1)
            for step, i in STEPS:
                if step == "x stats":
                    inv_std(0, i)
                if step == "emb + bo":
                    emb_plus_bo(i)
                if step == "x + beta":
                    x_with_beta(i)
                if step == "a + b2":
                    a_plus_b2(i)
                if step == "z1 stats":
                    inv_std(1, i)
                if step == "z2 stats":
                    inv_std(2, i)
                if step == "x1":
                    inv_std(3, i)
                if step == "weights low":
                    split_low(*divmod(i, 2))
                if step == "hidden split" and i < UNITS - 1:
                    hidden_low(i)
                if step == "band":
                    pool.wait_ge(ld_pos, 16)
                    for r in range(TPB):
                        pool.affine_select(out=pos[:, r, :], in_=pos[:, r, :], compare_op=ALU.is_gt, fill=0.0,
                                           base=SPAN + P * r, pattern=[[-1, T]],
                                           channel_multiplier=1).then_inc(band_done, 1)
                    for r in range(TPB):
                        pool.wait_ge(band_done, r + 1)
                        pool.affine_select(out=pos[:, r, :], in_=pos[:, r, :], compare_op=ALU.is_gt, fill=0.0,
                                           base=SPAN - P * r, pattern=[[1, T]],
                                           channel_multiplier=-1).then_inc(band_done, 1)
                if step == "exp":
                    pool.wait_ge(ld_rows, 16)
                    pool.wait_ge(gates_done, 2)
                    pool.tensor_scalar(tgamma[:, :], rows[:, R_GAMMA, :], tx[:, 0:1], None,
                                       ALU.mult).then_inc(pre_done, 1)
                    pool.tensor_scalar(tbeta[:, :], rows[:, R_BETA, :], tx[:, 0:1], None,
                                       ALU.mult).then_inc(pre_done, 1)
                    pool.tensor_tensor(rows[:, R_B2, :], rows[:, R_B2, :], rows[:, R_BETA, :],
                                       ALU.add).then_inc(pre_done, 1)

        @block.vector
        def _(dve):
            dve.memset(zeros[:, :], 0.0).then_inc(zeros_done, 1)

            def stats(norm, b, src):
                for i in range(TPB):
                    t = TPB * b + i
                    dve.bn_stats(st[:, norm, t, :], src[:, i, :]).then_inc(st_done[norm], 1)
                for i in range(TPB):
                    t = TPB * b + i
                    dve.wait_ge(st_done[norm], t + 1)
                    dve.bn_aggr(mv[:, norm, t, :], st[:, norm, t, :]).then_inc(mv_done[norm], 1)
                dve.wait_ge(mv_done[norm], TPB * (b + 1))
                dve.tensor_scalar(ve[:, norm, tok(b)], mv[:, norm, tok(b), 1], EPS, None,
                                  ALU.add).then_inc(ve_done[norm], 1)

            def mean(norm, t):
                return mv[:, norm, t, 0:1]

            def inv(norm, t):
                return rstd[:, norm, t:t + 1]

            def shift_of(norm, b):
                dve.wait_ge(rstd_done[norm], b + 1)
                dve.scalar_tensor_tensor(out=shift[:, norm, tok(b)], in0=mv[:, norm, tok(b), 0], scalar=-1.0,
                                         in1=rstd[:, norm, tok(b)], op0=ALU.mult,
                                         op1=ALU.mult).then_inc(shift_done[norm], 1)

            def ln_x_plus_ctx(b):
                dve.wait_ge(rstd_done[0], b + 1)
                for i in range(TPB):
                    t = TPB * b + i
                    dve.tensor_scalar(emb[:, t, :], x[:, t, :], mean(0, t), inv(0, t),
                                      ALU.subtract, ALU.mult).then_inc(xn_done, 1)
                if b % 2 == 0:
                    dve.wait_ge(ld_cx[b // 2], 16)
                dve.wait_ge(xn_done, TPB * (b + 1))
                dve.tensor_tensor(emb[:, tok(b), :], emb[:, tok(b), :], cx[:, tok(b), :],
                                  ALU.add).then_inc(emb_done, 1)

            def key_max(b):
                dve.wait_ge(kv_ready, b + 1)
                dve.tensor_reduce(kmax[:, b:b + 1], bank[AUX[b]][:, 0:T], AX.X, ALU.max).then_inc(kmax_done, 1)
                dve.wait_ge(kmax_done, b + 1)
                dve.tensor_scalar(kneg[:, b:b + 1], kmax[:, b:b + 1], cols[:, C_BK:C_BK + 1], -1.0,
                                  ALU.add, ALU.mult).then_inc(kneg_done, 1)
                dve.wait_ge(kneg_done, b + 1)
                dve.tensor_scalar(kbias[:, b:b + 1], kneg[:, b:b + 1], cols[:, C_BK:C_BK + 1], None,
                                  ALU.add).then_inc(kbias_done, 1)

            def key_times_value(b):
                dve.wait_ge(ek_done, b + 1)
                dve.scalar_tensor_tensor(out=ekvT[:, b, :], in0=bank[AUX[b]][:, T:2 * T],
                                         scalar=cols[:, C_BV:C_BV + 1], in1=ekT[:, b, :],
                                         op0=ALU.add, op1=ALU.mult).then_inc(ekv_done, 1)

            def aft_out(b):
                dve.wait_ge(aft_ready, b + 1)
                dve.scalar_tensor_tensor(out=y[:, b, :], in0=eq[:, b, :], scalar=1.0, in1=bank[MAIN[b]][:, T:2 * T],
                                         op0=ALU.add, op1=ALU.mult).then_inc(den_done, 1)
                dve.wait_ge(den_done, b + 1)
                for i in range(TPB):
                    cut = slice(P * i, P * i + P)
                    dve.reciprocal(y[:, b, cut], y[:, b, cut]).then_inc(rden_done, 1)
                    dve.wait_ge(rden_done, TPB * b + i + 1)
                    dve.tensor_tensor(y[:, b, cut], y[:, b, cut], bank[MAIN[b]][:, cut], ALU.mult).then_inc(y_done, 1)

            def tiles_in(psum):
                return psum[:, 0:T].rearrange("p (i d) -> p i d", i=TPB)

            def centred_z2_times_gamma(b):
                dve.wait_ge(mv_done[2], TPB * (b + 1))
                if b == 0:
                    dve.wait_ge(pre_done, 2)
                for i in range(TPB):
                    t = TPB * b + i
                    dve.scalar_tensor_tensor(out=ab[:, b, i, :], in0=ab[:, b, i, :],
                                             scalar=mean(2, t),
                                             in1=tgamma[:, :], op0=ALU.subtract, op1=ALU.mult).then_inc(n2g_done, 1)

            def gated_x1(b):
                dve.wait_ge(rstd_done[2], b + 1)
                dve.wait_ge(xtb_done, b + 1)
                for i in range(TPB):
                    t = TPB * b + i
                    dve.wait_ge(n2g_done, t + 1)
                    dve.scalar_tensor_tensor(out=x[:, t, :], in0=ab[:, b, i, :], scalar=inv(2, t),
                                             in1=x[:, t, :], op0=ALU.mult, op1=ALU.add).then_inc(x1_done, 1)
                dve.wait_ge(x1_done, TPB * (b + 1))
                stats(3, b, x[:, tok(b), :])

            def xfT_low(b):
                dve.wait_ge(xfThi_done, b + 1)
                dve.wait_ge(xfT_done, b + 1)
                dve.tensor_tensor(xfT_lo[:, T * b:T * b + T], xfT[:, T * b:T * b + T],
                                  f32(xfT_hi[:, T * b:T * b + T]), ALU.subtract).then_inc(xfTlo_done, 1)

            def pick_top2(h):
                dve.wait_ge(sc_ready, h + 1)
                dve.tensor_copy(sc[:, :, :], bank[SCORE_BANK[h]][:, 0:HT * E].rearrange("p (t e) -> p t e", e=E)) \
                   .then_inc(sc_done, 1)
                dve.wait_ge(sc_done, h + 1)
                for t in range(HT):
                    dve.max(top[:, t, :], sc[:, t, :]).then_inc(top_done, 1)
                for t in range(HT):
                    dve.wait_ge(top_done, HT * h + t + 1)
                    dve.max_index(topi[:, t, :], top[:, t, :], sc[:, t, :]).then_inc(topi_done, 1)
                dve.tensor_tensor(gap[:, :], top[:, :, 0], top[:, :, 1], ALU.subtract).then_inc(gap_done, 1)
                dve.wait_ge(topi_done, HT * (h + 1))
                dve.tensor_copy(topf[:, :, :], topi[:, :, 0:2]).then_inc(topf_done, 1)
                dve.wait_ge(topf_done, h + 1)
                for k in range(2):
                    dve.tensor_tensor(chosen[:, k, :, :],
                                      cols[:, C_IOTA:C_IOTA + E].unsqueeze(1).broadcast_to([P, HT, E]),
                                      topf[:, :, k:k + 1].broadcast_to([P, HT, E]),
                                      ALU.is_equal).then_inc(is_done, 1)

            def route(h):
                dve.wait_ge(tgap_done, h + 1)
                for k, slope in ((0, halftf), (1, neghalftf)):
                    dve.tensor_scalar(pw[:, k, :], tgap[:, :], slope[:, 0:1], halftf[:, 0:1],
                                      ALU.mult, ALU.add).then_inc(pw_done, 1)
                for k in range(2):
                    dve.wait_ge(is_done, 2 * h + k + 1)
                    dve.wait_ge(pw_done, 2 * h + k + 1)
                    dve.tensor_tensor(chosen[:, k, :, :], chosen[:, k, :, :],
                                      pw[:, k, :].unsqueeze(2).broadcast_to([P, HT, E]),
                                      ALU.mult).then_inc(chosen_done, 1)
                dve.wait_ge(chosen_done, 2 * (h + 1))
                dve.tensor_tensor(probs[:, :, :], chosen[:, 0, :, :], chosen[:, 1, :, :],
                                  ALU.add).then_inc(probs_done, 1)

            def copy_pT(h):
                dve.wait_ge(pT_ready, h + 1)
                if h:
                    dve.wait_ge(p_out, 16 * h)
                dve.tensor_copy(pT[:, :], bank[PT_BANK[h]][0:E, :]).then_inc(pT_done, 1)

            def hidden(u):
                dve.wait_ge(h2_ready, u + 1)
                for i, cut in enumerate(parts(u)):
                    dve.wait_ge(silu_done, u + i + 1)
                    dve.tensor_tensor(hid[:, u % HID_SLOTS, cut], hid[:, u % HID_SLOTS, cut],
                                      bank[H2_BANK[u % 2]][:, cut], ALU.mult).then_inc(hid_done, 1)

            def last_hidden_low():
                s = (UNITS - 1) % HID_SLOTS
                for i, cut in enumerate(parts(UNITS - 1)):
                    dve.wait_ge(hidhi_done, UNITS + i)
                    dve.tensor_tensor(hid_lo[:, s, cut], hid[:, s, cut], f32(hid_hi[:, s, cut]),
                                      ALU.subtract).then_inc(last_lo_done, 1)

            def add_expert(v):
                h, e = divmod(v, E)
                dve.wait_ge(p_back[e], 16 * (h + 1))
                for i, cut in enumerate(parts(ECH * v + ECH - 1)):
                    dve.wait_ge(y_ready, ECH * (v + 1) + i)
                    dve.tensor_tensor(pall[:, e, cut], pall[:, e, cut], y_bank(v, i)[:, cut],
                                      ALU.mult).then_inc(yp_done, 1)
                    if e == 0:
                        dve.wait_ge(x1T_done, 2 * (h + 1))
                    dve.wait_ge(yp_done, v + 1 + i)
                    if v:
                        dve.wait_ge(acc_done, v)
                    tokens = slice(HALF * h + cut.start, HALF * h + cut.stop)
                    dve.tensor_tensor(acc[:, tokens], acc[:, tokens], pall[:, e, cut], ALU.add).then_inc(acc_done, 1)

            for step, i in STEPS:
                if step == "x stats":
                    dve.wait_ge(ld_x[i], 16)
                    stats(0, i, x[:, tok(i), :])
                if step == "emb":
                    ln_x_plus_ctx(i)
                if step == "key maximum":
                    key_max(i)
                if step == "ekv":
                    key_times_value(i)
                if step == "y":
                    aft_out(i)
                if step == "z1 stats":
                    dve.wait_ge(attn_ready, i + 1)
                    dve.wait_ge(embb_done, i + 1)
                    dve.tensor_tensor(n1[:, i, :, :], tiles_in(bank[AUX[i]]), emb[:, tok(i), :],
                                      ALU.add).then_inc(z1_done, 1)
                    dve.wait_ge(z1_done, i + 1)
                    stats(1, i, n1[:, i, :, :])
                if step == "n1":
                    shift_of(1, i)
                if step == "z2 stats":
                    dve.wait_ge(ff2_ready, i + 1)
                    dve.wait_ge(ab_done, i + 1)
                    dve.tensor_tensor(ab[:, i, :, :], tiles_in(bank[AUX[i]]), ab[:, i, :, :],
                                      ALU.add).then_inc(z2_done, 1)
                    dve.wait_ge(z2_done, i + 1)
                    stats(2, i, ab[:, i, :, :])
                if step == "z2 times gamma":
                    centred_z2_times_gamma(i)
                if step == "x1":
                    gated_x1(i)
                if step == "xf":
                    shift_of(3, i)
                if step == "xf low":
                    xfT_low(i)
                if step == "top 2":
                    pick_top2(i)
                if step == "route":
                    route(i)
                if step == "probs transposed":
                    copy_pT(i)
                if step == "hidden":
                    hidden(i)
                if (step, i) == ("hidden split", UNITS - 1):
                    last_hidden_low()
                if step == "expert sum":
                    add_expert(i)
                if step == "exp":
                    for r in range(TPB):
                        dve.wait_ge(band_done, TPB + r + 1)
                        dve.tensor_reduce(wmax[:, r:r + 1], pos[:, r, :], AX.X, ALU.max).then_inc(wmax_done, 1)
                    dve.wait_ge(wmax_done, TPB)
                    dve.tensor_scalar(wneg[:, :], wmax[:, :], -1.0, None, ALU.mult).then_inc(wneg_done, 1)
                    dve.wait_ge(ld_cols, 16)
                    dve.tensor_scalar(negbq[:, :], cols[:, C_BQ:C_BQ + 1], -1.0, None, ALU.mult).then_inc(consts_done, 1)
                    dve.wait_ge(gates_done, 2)
                    dve.tensor_scalar(halftf[:, :], tf[:, :], 0.5, None, ALU.mult).then_inc(consts_done, 1)
                    dve.tensor_scalar(neghalftf[:, :], tf[:, :], -0.5, None, ALU.mult).then_inc(consts_done, 1)

        @block.scalar
        def _(act):
            act.dma_start(ident[:, :], ident_in).then_inc(ld_ident, 16)
            act.dma_start(cols[:, :], cols_in).then_inc(ld_cols, 16)
            act.dma_start(pos[:, :, :], pos_in).then_inc(ld_pos, 16)
            act.dma_start(rows[:, :, :], rows_in).then_inc(ld_rows, 16)
            act.dma_start(gate[:, :], gate_in).then_inc(ld_gate, 16)

            def copy(dst, src):
                return act.activation(dst, src, ACT.Copy)

            def split_high(e):
                act.wait_ge(ld_raw[e % RAW_SLOTS], 16 * (e // RAW_SLOTS + 1))
                copy(ex_hi[:, e, :], raw[:, e % RAW_SLOTS, :]).then_inc(whi_done, 1)

            def normalize(norm, b, dst, src, done):
                act.wait_ge(shift_done[norm], b + 1)
                for i in range(TPB):
                    t = TPB * b + i
                    act.activation(dst(i), src(i), ACT.Identity, bias=shift[:, norm, t:t + 1],
                                   scale=rstd[:, norm, t:t + 1]).then_inc(done, 1)

            def copy_embT(b):
                act.wait_ge(embT_ready, b + 1)
                copy(embT[:, b, :], bank[MAIN[b]][:, 0:T]).then_inc(embT_done, 1)

            def exp_key(b):
                act.wait_ge(kbias_done, b + 1)
                act.activation(ekT[:, b, :], bank[AUX[b]][:, 0:T], ACT.Exp,
                               bias=kbias[:, b:b + 1]).then_inc(ek_done, 1)

            def exp_query(b):
                if b == 0:
                    act.wait_ge(consts_done, 1)
                act.wait_ge(q_ready, b + 1)
                act.activation(eq[:, b, :], bank[MAIN[b]][:, 0:T], ACT.Exp, bias=negbq[:, 0:1],
                               scale=-1.0).then_inc(eq_done, 1)

            def copy_kv(b):
                act.wait_ge(kvT_ready, b + 1)
                copy(kv[:, b, :, :, :].rearrange("p i k d -> p (i k d)"),
                     bank[AUX[b]][:, :]).then_inc(kv_done, 1)

            def a_transposed(b):
                act.wait_ge(n1T_ready, b + 1)
                act.activation(aT[:, b, :], bank[MAIN[b]][:, T:2 * T], ACT.Identity, bias=cols[:, C_BETA:C_BETA + 1],
                               scale=cols[:, C_GAMMA:C_GAMMA + 1]).then_inc(aT_done, 1)

            def relu(b, s):
                act.wait_ge(ff1_ready[b], s + 1)
                for c in range(2):
                    act.activation(hr[:, b, 2 * s + c, :], bank[[AUX, MAIN][s][b]][:, T * c:T * c + T], ACT.Relu,
                                   bias=cols[:, C_B1 + 2 * s + c:C_B1 + 2 * s + c + 1]).then_inc(hr_done[b], 1)

            def xfT_high(b):
                act.wait_ge(xfT_ready, b + 1)
                copy(xfT_hi[:, T * b:T * b + T], bank[MAIN[b]][:, 0:T]).then_inc(xfThi_done, 1)
                copy(xfT[:, T * b:T * b + T], bank[MAIN[b]][:, 0:T]).then_inc(xfT_done, 1)
                copy(acc[:, T * b:T * b + T], bank[AUX[b]][:, T:2 * T]).then_inc(x1T_done, 1)

            def silu(u):
                act.wait_ge(h1_ready, u + 1)
                if u >= HID_SLOTS:
                    act.wait_ge(hidlo_done, u - HID_SLOTS + 1)
                for cut in parts(u):
                    act.activation(hid[:, u % HID_SLOTS, cut], bank[H1_BANK[u % 2]][:, cut],
                                   ACT.Silu).then_inc(silu_done, 1)

            def hidden_high(u):
                if u >= HID_SLOTS:
                    act.wait_ge(y_ready, u - HID_SLOTS + 1)
                for i, cut in enumerate(parts(u)):
                    act.wait_ge(hid_done, u + i + 1)
                    copy(hid_hi[:, u % HID_SLOTS, cut], hid[:, u % HID_SLOTS, cut]).then_inc(hidhi_done, 1)

            for step, i in STEPS:
                if step == "n1":
                    normalize(1, i, lambda k: n1[:, i, k, :], lambda k: n1[:, i, k, :], n1_done)
                if step == "xf":
                    normalize(3, i, lambda k: xf[:, i, k, :], lambda k: x[:, TPB * i + k, :], xf_done)
                if step == "keys and values":
                    copy_embT(i)
                if step == "key maximum":
                    exp_key(i)
                if step == "query":
                    exp_query(i)
                if step == "ek and ekv transposed":
                    copy_kv(i)
                if step == "a":
                    a_transposed(i)
                if step == "feed forward 0":
                    relu(i, 0)
                if step == "feed forward 1":
                    relu(i, 1)
                if step == "xf transposed":
                    xfT_high(i)
                if step == "top 2":
                    act.wait_ge(gap_done, i + 1)
                    act.activation(tgap[:, :], gap[:, :], ACT.Tanh, scale=0.5).then_inc(tgap_done, 1)
                if step == "weights high":
                    split_high(i)
                if step == "hidden":
                    silu(i)
                if step == "hidden split":
                    hidden_high(i)
                if step == "band":
                    act.wait_ge(ld_cols, 16)
                    act.activation(tx[:, :], cols[:, C_GX:C_GX + 1], ACT.Tanh).then_inc(gates_done, 1)
                    act.activation(tf[:, :], cols[:, C_GF:C_GF + 1], ACT.Tanh).then_inc(gates_done, 1)
                if step == "exp":
                    act.wait_ge(wneg_done, 1)
                    for r in range(TPB):
                        act.activation(pos[:, r, :], pos[:, r, :], ACT.Exp, bias=wneg[:, r:r + 1]).then_inc(ew_done, 1)
                if step == "ew":
                    act.wait_ge(ewT_ready, 1)
                    copy(ewT[:, :, :].rearrange("p i t -> p (i t)"), bank[EW_BANK][:, :]).then_inc(ewT_done, 1)
            act.wait_ge(acc_done, E)
            act.dma_start(out[:, 0:HALF], acc[:, 0:HALF]).then_inc(out_done, 16)

        @block.tensor
        def _(pe):
            def product(dst, w_hi, w_lo, m_hi, m_lo, first=True, last=True):
                pe.matmul(dst, w_hi, m_hi, start=first, stop=False)
                pe.matmul(dst, w_hi, m_lo, start=False, stop=False)
                return pe.matmul(dst, w_lo, m_hi, start=False, stop=last)

            def transpose_emb(b):
                pe.wait_ge(emb_done, b + 1)
                for i in range(TPB):
                    mm = pe.transpose(bank[MAIN[b]][:, P * i:P * i + P], emb[:, TPB * b + i, :], ident[:, :])
                mm.then_inc(embT_ready, 1)

            def project(dst, w, b):
                return pe.matmul(dst, wa[:, w, :], embT[:, b, :], start=True, stop=True)

            def keys_values(b):
                if b == 0:
                    pe.wait_ge(ld_wa, 16)
                pe.wait_ge(embT_done, b + 1)
                project(bank[AUX[b]][:, 0:T], WK, b)
                project(bank[AUX[b]][:, T:2 * T], WV, b).then_inc(kv_ready, 1)

            def queries(b):
                if AUX[b] == MAIN[b]:
                    pe.wait_ge(ekv_done, b + 1)
                project(bank[MAIN[b]][:, 0:T], WQ, b).then_inc(q_ready, 1)

            def kvT(b):
                pe.wait_ge(ekv_done, b + 1)
                if AUX[b] == MAIN[b]:
                    pe.wait_ge(eq_done, b + 1)
                for i in range(TPB):
                    for k, src in enumerate((ekvT, ekT)):
                        mm = pe.transpose(bank[AUX[b]][:, P * (2 * i + k):P * (2 * i + k + 1)],
                                          src[:, b, P * i:P * i + P], ident[:, :])
                mm.then_inc(kvT_ready, 1)

            def aft(b):
                if b == 0:
                    pe.wait_ge(ewT_done, 1)
                pe.wait_ge(kv_done, b + 1)
                pe.wait_ge(eq_done, b + 1)
                for k in (1, 0):
                    for i in range(TPB):
                        mm = pe.matmul(bank[MAIN[b]][:, T * k:T * k + T], kv[:, b, i, k, :], ewT[:, i, :],
                                       start=(i == 0), stop=(i == TPB - 1))
                mm.then_inc(aft_ready, 1)

            def attention(b):
                for i in range(TPB):
                    pe.wait_ge(y_done, TPB * b + (TPB if AUX[b] == MAIN[b] else i + 1))
                    mm = pe.matmul(bank[AUX[b]][:, P * i:P * i + P], y[:, b, P * i:P * i + P], wa[:, WO, :],
                                   start=True, stop=True)
                mm.then_inc(attn_ready, 1)

            def n1T(b):
                pe.wait_ge(n1_done, TPB * (b + 1))
                for i in range(TPB):
                    mm = pe.transpose(bank[MAIN[b]][:, T + P * i:T + P * i + P], n1[:, b, i, :], ident[:, :])
                mm.then_inc(n1T_ready, 1)

            def ff1(b, s):
                if s == 0:
                    if b == 0:
                        pe.wait_ge(ld_w1, 16)
                    pe.wait_ge(aT_done, b + 1)
                elif AUX[b] == MAIN[b]:
                    pe.wait_ge(hr_done[b], HCH // 2)
                for c in range(2):
                    cut = slice(P * (2 * s + c), P * (2 * s + c) + P)
                    mm = pe.matmul(bank[[AUX, MAIN][s][b]][:, T * c:T * c + T], w1[:, cut], aT[:, b, :],
                                   start=True, stop=True)
                mm.then_inc(ff1_ready[b], 1)

            def ff2(b):
                if b == 0:
                    pe.wait_ge(ld_w2, 16)
                pe.wait_ge(hr_done[b], HCH)
                for i in range(TPB):
                    for c in range(HCH):
                        mm = pe.matmul(bank[AUX[b]][:, P * i:P * i + P], hr[:, b, c, P * i:P * i + P], w2[:, c, :],
                                       start=(c == 0), stop=(c == HCH - 1))
                mm.then_inc(ff2_ready, 1)

            def xf_x1_T(b):
                pe.wait_ge(xf_done, TPB * (b + 1))
                for i in range(TPB):
                    pe.transpose(bank[AUX[b]][:, T + P * i:T + P * i + P], x[:, TPB * b + i, :], ident[:, :])
                for i in range(TPB):
                    mm = pe.transpose(bank[MAIN[b]][:, P * i:P * i + P], xf[:, b, i, :], ident[:, :])
                mm.then_inc(xfT_ready, 1)

            def scores(h):
                if h == 0:
                    pe.wait_ge(ld_gate, 16)
                pe.wait_ge(xfT_done, 2 * (h + 1))
                if SCORE_BANK[h] in MAIN:
                    pe.wait_ge(x1T_done, 2 * (h + 1))
                for t in range(HT):
                    cut = slice(HALF * h + P * t, HALF * h + P * t + P)
                    mm = pe.matmul(bank[SCORE_BANK[h]][:, E * t:E * t + E], xfT[:, cut], gate[:, :],
                                   start=True, stop=True)
                mm.then_inc(sc_ready, 1)

            def probsT(h):
                pe.wait_ge(probs_done, h + 1)
                for t in range(HT):
                    mm = pe.transpose(bank[PT_BANK[h]][0:E, P * t:P * t + P], probs[:, t, :], ident[:, :])
                mm.then_inc(pT_ready, 1)

            def expert_in(u):
                h, e, c = u // UPH, u % UPH // ECH, u % ECH
                pe.wait_ge(wlo_done, 2 * e + 1)
                pe.wait_ge(xfTlo_done, 2 * (h + 1))
                pe.wait_ge(x1T_done, 2 * (h + 1))
                tokens = slice(HALF * h, HALF * h + HALF)
                for part, (banks, freed, ready) in enumerate(((H1_BANK, silu_done, h1_ready),
                                                              (H2_BANK, hid_done, h2_ready))):
                    if u >= 2:
                        pe.wait_ge(freed, u - 1)
                    cut = slice(EH * part + P * c, EH * part + P * c + P)
                    product(bank[banks[u % 2]][:, :], ex_hi[:, e, cut], ex_lo[:, e, cut],
                            xfT_hi[:, tokens], xfT_lo[:, tokens]).then_inc(ready, 1)

            def expert_out(u):
                e, c, v = u % UPH // ECH, u % ECH, u // ECH
                pe.wait_ge(wlo_done, 2 * (e + 1))
                if v == 1:
                    pe.wait_ge(pT_done, 1)
                if v >= 2 and c == 0:
                    pe.wait_ge(yp_done, v - 1)
                cut = slice(2 * EH + D * c, 2 * EH + D * c + D)
                if u < UNITS - 1:
                    pe.wait_ge(hidlo_done, u + 1)
                for i, tokens in enumerate(parts(u + ECH - 1 - c)):
                    if u == UNITS - 1:
                        pe.wait_ge(last_lo_done, i + 1)
                    mm = product(y_bank(v, i)[:, tokens], ex_hi[:, e, cut], ex_lo[:, e, cut],
                                 hid_hi[:, u % HID_SLOTS, tokens], hid_lo[:, u % HID_SLOTS, tokens],
                                 first=(c == 0), last=(c == ECH - 1))
                    if u == UNITS - 1 or i + 1 == len(parts(u + ECH - 1 - c)):
                        mm.then_inc(y_ready, 1)

            pe.wait_ge(zeros_done, 1)
            for _ in range(WARM_UPS):
                pe.matmul(bank[Y_BANK[0]][:, 0:T], zeros[:, 0:P], zeros[:, :], start=True, stop=True)
            pe.wait_ge(ld_ident, 16)
            for step, i in STEPS:
                if step == "emb transposed":
                    transpose_emb(i)
                if step == "keys and values":
                    keys_values(i)
                if step == "query":
                    queries(i)
                if step == "ek and ekv transposed":
                    kvT(i)
                if step == "aft":
                    aft(i)
                if step == "attention":
                    attention(i)
                if step == "a":
                    n1T(i)
                if step == "feed forward 0":
                    ff1(i, 0)
                if step == "feed forward 1":
                    ff1(i, 1)
                if step == "feed forward 2":
                    ff2(i)
                if step == "xf transposed":
                    xf_x1_T(i)
                if step == "scores":
                    scores(i)
                if step == "probs transposed":
                    probsT(i)
                if step == "unit in":
                    expert_in(i)
                if step == "unit out":
                    expert_out(i)
                if step == "exp":
                    pe.wait_ge(ew_done, TPB)
                    for k in range(TPB):
                        for r in range(TPB):
                            mm = pe.transpose(bank[EW_BANK][:, T * k + P * r:T * k + P * r + P],
                                              pos[:, r, P * k:P * k + P], ident[:, :])
                    mm.then_inc(ewT_ready, 1)


def kernel(**inputs):
    import numpy as np
    import concourse.bacc as bacc
    from concourse import mybir as mb
    from concourse.bass_utils import run_bass_kernel_spmd

    g = {k: np.asarray(v) for k, v in inputs.items()}
    a = {k[len("L0_xattn_"):]: v for k, v in g.items() if k.startswith("L0_xattn_")}
    f = {k[len("L0_ffn_"):]: v for k, v in g.items() if k.startswith("L0_ffn_")}

    def token_rows(v):
        return v.reshape(TILES, P, D).transpose(1, 0, 2)

    def on_partitions(v):
        return v.reshape(-1, P).T

    iota = np.tile(np.arange(E, dtype=np.float32), (P, 1))
    cols = np.concatenate([on_partitions(a[n]) for n in ("bq", "bk", "bv", "gamma", "beta", "b1")]
                          + [np.tile(g[n].reshape(1, 1), (P, 1)) for n in ("g_xattn", "g_ffn")] + [iota], axis=1)
    rows = np.stack([np.tile(a[n], (P, 1)) for n in ("gamma", "beta", "bo", "b2")], axis=1)
    experts = np.concatenate([f["w12"].transpose(2, 0, 1),
                              f["w3"].reshape(E, D, ECH, P).transpose(3, 0, 2, 1).reshape(P, E, ECH * D)], axis=2)
    feeds = {
        "x_in": token_rows(g["x"]),
        "ctx_in": token_rows(g["ctx_1024"]),
        "ident_in": np.eye(P, dtype=np.float32),
        "cols_in": cols,
        "rows_in": rows,
        "pos_in": a["pos_bias"].reshape(TPB, P, T).transpose(1, 0, 2),
        "wa_in": np.stack([a[n] for n in ("wq", "wk", "wv", "wo")], axis=1),
        "w1_in": a["w1"],
        "w2_in": a["w2"].reshape(HCH, P, D).transpose(1, 0, 2),
        "gate_in": f["gate_w"].T,
        "experts_in": experts,
    }
    nc = bacc.Bacc("TRN2", target_bir_lowering=False, num_devices=1)
    feeds = {k: np.ascontiguousarray(v) for k, v in feeds.items()}
    aps = [nc.dram_tensor(k, v.shape, mb.dt.from_np(v.dtype), kind="ExternalInput").ap() for k, v in feeds.items()]
    out = nc.dram_tensor("out", (P, N), mb.dt.float32, kind="ExternalOutput").ap()
    build(nc, *aps, out)
    done = run_bass_kernel_spmd(nc, [feeds], core_ids=[0])
    return done.results[0]["out"].T.reshape(B, T, D)
```
